# Optimizing a Trainium2 kernel written in Bass

```python
import numpy as np
import jax
import jax.numpy as jnp

def _softmax(x, axis=-1):
    return jax.nn.softmax(x, axis=axis)

def _gelu(x):
    return jax.nn.gelu(x, approximate=True)

def _silu(x):
    return jax.nn.silu(x)

def _sigmoid(x):
    return jax.nn.sigmoid(x)

def _layernorm(x, axis=-1, eps=1e-05):
    m = jnp.mean(x, axis=axis, keepdims=True)
    v = jnp.var(x, axis=axis, keepdims=True)
    return (x - m) / jnp.sqrt(v + eps)

def _scatter_add(tgt, idx, src, axis=0):
    return tgt.at[idx].add(src)

def _segment_sum(src, seg, n):
    return jax.ops.segment_sum(src, seg, n)
kernel_name = 'mk_seq_preln_d1_jaxref_r8_a6e762'

def setup_inputs(seed: int=0):
    np.random.seed(seed)
    _w = jnp.asarray

    def _L0_attn_setup():
        import jax, jax.numpy as jnp
        import numpy as np
        B, S, D = (4, 512, 128)
        H = 16
        HD = D // H

        def feature_map(x):
            return jnp.exp(-jnp.square(x) * 0.5)
        key = jax.random.key(seed)
        ks = jax.random.split(key, 9)
        s = 1.0 / np.sqrt(D)
        return {'x': jax.random.normal(ks[0], (B, S, D), dtype=jnp.float32), 'Wq': jax.random.normal(ks[1], (D, D), dtype=jnp.float32) * s, 'bq': jax.random.normal(ks[2], (D,), dtype=jnp.float32) * s, 'Wk': jax.random.normal(ks[3], (D, D), dtype=jnp.float32) * s, 'bk': jax.random.normal(ks[4], (D,), dtype=jnp.float32) * s, 'Wv': jax.random.normal(ks[5], (D, D), dtype=jnp.float32) * s, 'bv': jax.random.normal(ks[6], (D,), dtype=jnp.float32) * s, 'Wo': jax.random.normal(ks[7], (D, D), dtype=jnp.float32) * s, 'bo': jax.random.normal(ks[8], (D,), dtype=jnp.float32) * s}
    _L0_attn_in = _L0_attn_setup()

    def _L0_ffn_setup():
        import jax, jax.numpy as jnp
        import numpy as np
        EMB = 128
        HID = 256
        HEADS = 16
        HEAD_DIM = EMB // HEADS
        EXPERTS = 8
        TOPK = 2
        EPS = 1e-05

        def layernorm(x, scale, shift):
            mean = jnp.mean(x, axis=-1, keepdims=True)
            var = jnp.mean((x - mean) ** 2, axis=-1, keepdims=True)
            return scale * (x - mean) / jnp.sqrt(var + EPS) + shift

        def attention(x, wq, wk, wv, wo, bo):
            b, t, _ = x.shape
            q = (x @ wq).reshape(b, t, HEADS, HEAD_DIM)
            k = (x @ wk).reshape(b, t, HEADS, HEAD_DIM)
            v = (x @ wv).reshape(b, t, HEADS, HEAD_DIM)
            scores = jnp.einsum('bqhd,bkhd->bhqk', q, k)
            mask = jnp.arange(t)[:, None] < jnp.arange(t)[None, :]
            scores = jnp.where(mask, -jnp.inf, scores)
            attn = jax.nn.softmax(scores / np.sqrt(HEAD_DIM), axis=-1)
            ctx = jnp.einsum('bhqk,bkhd->bqhd', attn, v).reshape(b, t, EMB)
            return ctx @ wo + bo

        def moe_ff(x, gate_w, w1, w2, w3):
            b, t, d = x.shape
            xf = x.reshape(b * t, d)
            scores = xf @ gate_w
            topk_scores, topk_idx = jax.lax.top_k(scores, TOPK)
            topk_probs = jax.nn.softmax(topk_scores, axis=-1)
            weight = jnp.sum(jax.nn.one_hot(topk_idx, EXPERTS, dtype=xf.dtype) * topk_probs[..., None], axis=1)
            h = jax.nn.silu(jnp.einsum('td,edh->eth', xf, w1)) * jnp.einsum('td,edh->eth', xf, w2)
            out_e = jnp.einsum('eth,ehd->etd', h, w3)
            out = jnp.einsum('etd,te->td', out_e, weight)
            return out.reshape(b, t, d)
        key = jax.random.key(seed)
        ks = jax.random.split(key, 12)
        s = lambda k, shape, fan: jax.random.normal(k, shape, jnp.float32) / np.sqrt(fan)
        return {'x': jax.random.normal(ks[0], (2, 256, EMB), jnp.float32), 'ln1_scale': jnp.ones((EMB,), jnp.float32), 'ln1_shift': jnp.zeros((EMB,), jnp.float32), 'wq': s(ks[1], (EMB, EMB), EMB), 'wk': s(ks[2], (EMB, EMB), EMB), 'wv': s(ks[3], (EMB, EMB), EMB), 'wo': s(ks[4], (EMB, EMB), EMB), 'bo': jnp.zeros((EMB,), jnp.float32), 'ln2_scale': jnp.ones((EMB,), jnp.float32), 'ln2_shift': jnp.zeros((EMB,), jnp.float32), 'gate_w': s(ks[5], (EMB, EXPERTS), EMB), 'w1': s(ks[6], (EXPERTS, EMB, HID), EMB), 'w2': s(ks[7], (EXPERTS, EMB, HID), EMB), 'w3': s(ks[8], (EXPERTS, HID, EMB), HID)}
    _L0_ffn_in = _L0_ffn_setup()
    _d = {'L0_attn_x': _L0_attn_in['x'], 'L0_attn_Wq': _L0_attn_in['Wq'], 'L0_attn_bq': _L0_attn_in['bq'], 'L0_attn_Wk': _L0_attn_in['Wk'], 'L0_attn_bk': _L0_attn_in['bk'], 'L0_attn_Wv': _L0_attn_in['Wv'], 'L0_attn_bv': _L0_attn_in['bv'], 'L0_attn_Wo': _L0_attn_in['Wo'], 'L0_attn_bo': _L0_attn_in['bo'], 'L0_ffn_ln1_scale': _L0_ffn_in['ln1_scale'], 'L0_ffn_ln1_shift': _L0_ffn_in['ln1_shift'], 'L0_ffn_wq': _L0_ffn_in['wq'], 'L0_ffn_wk': _L0_ffn_in['wk'], 'L0_ffn_wv': _L0_ffn_in['wv'], 'L0_ffn_wo': _L0_ffn_in['wo'], 'L0_ffn_bo': _L0_ffn_in['bo'], 'L0_ffn_ln2_scale': _L0_ffn_in['ln2_scale'], 'L0_ffn_ln2_shift': _L0_ffn_in['ln2_shift'], 'L0_ffn_gate_w': _L0_ffn_in['gate_w'], 'L0_ffn_w1': _L0_ffn_in['w1'], 'L0_ffn_w2': _L0_ffn_in['w2'], 'L0_ffn_w3': _L0_ffn_in['w3']}
    _x0 = _d['L0_attn_x']
    _d['L0_attn_x'] = jax.random.normal(jax.random.fold_in(jax.random.key(seed), 1), (4, 1024, 128), dtype=_x0.dtype)
    del _x0
    return _d

def reference(L0_attn_x, L0_attn_Wq, L0_attn_bq, L0_attn_Wk, L0_attn_bk, L0_attn_Wv, L0_attn_bv, L0_attn_Wo, L0_attn_bo, L0_ffn_ln1_scale, L0_ffn_ln1_shift, L0_ffn_wq, L0_ffn_wk, L0_ffn_wv, L0_ffn_wo, L0_ffn_bo, L0_ffn_ln2_scale, L0_ffn_ln2_shift, L0_ffn_gate_w, L0_ffn_w1, L0_ffn_w2, L0_ffn_w3):

    def _L0_attn_ref(x, Wq, bq, Wk, bk, Wv, bv, Wo, bo):
        import jax, jax.numpy as jnp
        import numpy as np
        B, S, D = (4, 512, 128)
        H = 16
        HD = D // H

        def feature_map(x):
            return jnp.exp(-jnp.square(x) * 0.5)
        b, s, _ = x.shape
        q = feature_map((x @ Wq + bq).reshape(b, s, H, HD))
        k = feature_map((x @ Wk + bk).reshape(b, s, H, HD))
        v = (x @ Wv + bv).reshape(b, s, H, HD)
        coeff = jnp.sum(q * k, axis=-1, keepdims=True)
        qkv = coeff * v
        out = qkv.reshape(b, s, H * HD)
        return out @ Wo + bo

    def _L0_ffn_ref(x, ln1_scale, ln1_shift, wq, wk, wv, wo, bo, ln2_scale, ln2_shift, gate_w, w1, w2, w3):
        import jax, jax.numpy as jnp
        import numpy as np
        EMB = 128
        HID = 256
        HEADS = 16
        HEAD_DIM = EMB // HEADS
        EXPERTS = 8
        TOPK = 2
        EPS = 1e-05

        def layernorm(x, scale, shift):
            mean = jnp.mean(x, axis=-1, keepdims=True)
            var = jnp.mean((x - mean) ** 2, axis=-1, keepdims=True)
            return scale * (x - mean) / jnp.sqrt(var + EPS) + shift

        def attention(x, wq, wk, wv, wo, bo):
            b, t, _ = x.shape
            q = (x @ wq).reshape(b, t, HEADS, HEAD_DIM)
            k = (x @ wk).reshape(b, t, HEADS, HEAD_DIM)
            v = (x @ wv).reshape(b, t, HEADS, HEAD_DIM)
            scores = jnp.einsum('bqhd,bkhd->bhqk', q, k)
            mask = jnp.arange(t)[:, None] < jnp.arange(t)[None, :]
            scores = jnp.where(mask, -jnp.inf, scores)
            attn = jax.nn.softmax(scores / np.sqrt(HEAD_DIM), axis=-1)
            ctx = jnp.einsum('bhqk,bkhd->bqhd', attn, v).reshape(b, t, EMB)
            return ctx @ wo + bo

        def moe_ff(x, gate_w, w1, w2, w3):
            b, t, d = x.shape
            xf = x.reshape(b * t, d)
            scores = xf @ gate_w
            topk_scores, topk_idx = jax.lax.top_k(scores, TOPK)
            topk_probs = jax.nn.softmax(topk_scores, axis=-1)
            weight = jnp.sum(jax.nn.one_hot(topk_idx, EXPERTS, dtype=xf.dtype) * topk_probs[..., None], axis=1)
            h = jax.nn.silu(jnp.einsum('td,edh->eth', xf, w1)) * jnp.einsum('td,edh->eth', xf, w2)
            out_e = jnp.einsum('eth,ehd->etd', h, w3)
            out = jnp.einsum('etd,te->td', out_e, weight)
            return out.reshape(b, t, d)
        h = layernorm(x, ln1_scale, ln1_shift)
        x = x + attention(h, wq, wk, wv, wo, bo)
        h = layernorm(x, ln2_scale, ln2_shift)
        x = x + moe_ff(h, gate_w, w1, w2, w3)
        return x
    x = L0_attn_x
    x = x + _L0_attn_ref(_layernorm(x, axis=-1), L0_attn_Wq, L0_attn_bq, L0_attn_Wk, L0_attn_bk, L0_attn_Wv, L0_attn_bv, L0_attn_Wo, L0_attn_bo)
    x = x + _L0_ffn_ref(_layernorm(x, axis=-1), L0_ffn_ln1_scale, L0_ffn_ln1_shift, L0_ffn_wq, L0_ffn_wk, L0_ffn_wv, L0_ffn_wo, L0_ffn_bo, L0_ffn_ln2_scale, L0_ffn_ln2_shift, L0_ffn_gate_w, L0_ffn_w1, L0_ffn_w2, L0_ffn_w3)
    return x

_drawn_inputs = setup_inputs


def setup_inputs(seed=0):
    import zlib

    import numpy as np

    out = dict(_drawn_inputs(seed))
    spreads = {'L0_ffn_ln1_scale': (1.0, 0.545),
     'L0_ffn_ln1_shift': (0.0, 0.1),
     'L0_ffn_bo': (0.0, 0.269),
     'L0_ffn_ln2_scale': (1.0, 0.2),
     'L0_ffn_ln2_shift': (0.0, 0.271)}
    factors = {}
    for name, (base, spread) in spreads.items():
        noise = np.random.default_rng([zlib.crc32(name.encode()), seed]).standard_normal(out[name].shape)
        drawn = base * np.exp(spread * noise) if base else spread * noise
        out[name] = jnp.asarray(drawn.astype(out[name].dtype))
    for name, factor in factors.items():
        out[name] = (out[name] * factor).astype(out[name].dtype)
    return out
```

```python
import concourse.bass as bass
from concourse import mybir
from contextlib import ExitStack


def preln_layer_kernel(nc: bass.Bass, x, Wq, bq, Wk, bk, Wv, bv, Wo, bo,
                       ln1_scale, ln1_shift, wq, wk, wv, wo, fbo,
                       ln2_scale, ln2_shift, gate_w, w1, w2, w3, out):
    fp32 = mybir.dt.float32
    bf16 = mybir.dt.bfloat16
    ALU = mybir.AluOpType
    ACT = mybir.ActivationFunctionType
    X = mybir.AxisListType.X

    P = 128
    B, S, D = x.shape
    NT = B * S // P
    H, HD = 16, 8
    EX, HID = w1.shape[0], w1.shape[2]
    EPS = 1e-5
    HG = 4
    NG = B * H // HG
    TB = S // P
    Q = 512
    SCALE = HD ** -0.5
    MASKED = -3.0e38
    KS = 96
    KM = 98
    PARTS = [(0, 0), (0, 1), (0, 2), (1, 0), (1, 1), (2, 0)]
    CH = 2
    NC = NT // CH
    W = CH * P

    def wait_alone(eng, semaphore, count):
        eng.wait_ge(semaphore, count)
        if not isinstance(count, int):
            eng.sem_inc(passed)

    MAXU = []
    for c in (1, 0):
        for t in range(4 * c, TB):
            w = min(Q, (t + 1) * P - c * Q)
            n = {128: 4, 256: 2}.get(w, 1)
            MAXU += [(t, c, i, n, w) for i in range(0, HG, n)]
    EXPG = []
    for c in (1, 0):
        for j in range(4 * (c + 1)):
            w = (c + 1) * Q - max(c * Q, j * P)
            EXPG.append((c, j, w, j >= 4 * c))
    EXPU = [(n, i, {128: 4, 256: 2}.get(EXPG[n][2], 1)) for n in range(len(EXPG))
            for i in range(0, HG, {128: 4, 256: 2}.get(EXPG[n][2], 1))]
    NMU, NEU, NEG = len(MAXU), len(EXPU), len(EXPG)
    LATE_UNITS = sum(1 for u in EXPU if EXPG[u[0]][0] == 1)
    LATE_KEYS = sum(1 for u in MAXU if u[1] == 1)
    NDG = sum(g[3] for g in EXPG)
    UNITS_UNTIL = [sum(1 for u in EXPU if u[0] <= n) for n in range(NEG)]
    DIAG_UNTIL = [sum(g[3] for g in EXPG[:n + 1]) for n in range(NEG)]

    def since(ring, u):
        before = [v for v in range(u) if ring[v] == ring[u]]
        if before:
            return before[-1] + 1
        return max(v for v in range(len(ring)) if ring[v] == ring[u]) + 1 - len(ring)


    PV_LAG = 2
    MAX_BY = 29

    def turn_order():
        order, m, e = [], 0, 0
        for n in range(NEG):
            if n == PV_LAG:
                order.append(("copy_ctx", 1))
            if n == 8 + PV_LAG:
                order.append(("copy_ctx", 0))
            for u in [u for u in EXPU if u[0] == n]:
                order.append(("exp", e))
                e += 1
                while m < min(NMU, e * NMU // MAX_BY):
                    order.append(("max", m))
                    m += 1
            if m == NMU and ("negate_max", 0) not in order:
                order.append(("negate_max", 0))
                turn_at = n + 1
            order.append(("pv", n - PV_LAG))
            if ("negate_max", 0) in order and n == turn_at:
                order.append(("turn_max", 0))
            if n == PV_LAG + 1:
                order.append(("turn_ctx", 1))
            if n == NEG - 1:
                order.append(("turn_ctx", 0))
        return order
    TURN = turn_order()
    EXPB = [e % 3 for e in range(NEU)]
    MAXB = [m % 3 for m in range(NMU)]

    ctx = ExitStack()
    with ctx:
        def sb(name, shape, dt=fp32):
            return ctx.enter_context(nc.sbuf_tensor(name, shape, dt))

        def sem(name):
            return ctx.enter_context(nc.semaphore(name))

        banks = [ctx.enter_context(nc.psum_tensor(f"bank{i}", [P, Q], fp32)) for i in range(8)]
        qparts = nc.dram_tensor("qparts", (2, B, H // HG, 3, HD, HG * S // 2), bf16, kind="Internal").ap()
        kparts = nc.dram_tensor("kparts", (2, B, H // HG, 3, HD, HG * S // 2), bf16, kind="Internal").ap()

        xs = sb("xs", [P, NT, D])
        vs = sb("vs", [P, NT, D])
        att = sb("att", [P, NT, D])
        stats1 = sb("stats1", [P, NT, 2])
        rstd1 = sb("rstd1", [P, NT])
        ident = sb("ident", [P, P])
        identb = sb("identb", [P, P], bf16)
        headones = sb("headones", [P, P])
        maskb = sb("maskb", [P, P], bf16)
        power = sb("power", [P, CH])
        Wq_s, Wk_s, Wv_s, Wo_s = (sb(n, [P, D]) for n in ("Wq_s", "Wk_s", "Wv_s", "Wo_s"))
        wq_s, wk_s, wv_s, wo_s = (sb(n, [P, D]) for n in ("wq_s", "wk_s", "wv_s", "wo_s"))
        cols = sb("cols", [P, 7])
        bq_c, bk_c, bv_c, s1_c, t1_c, s2_c, t2_c = (cols[:, i:i + 1] for i in range(7))
        bo_r = sb("bo_r", [P, D])
        fbo_r = sb("fbo_r", [P, D])

        passed = sem("passed")
        w_in = sem("weights_loaded")
        consts = sem("consts_ready")

        with ExitStack() as mix, nc.Block() as block:
            def mb(name, shape, dt=fp32):
                return mix.enter_context(nc.sbuf_tensor(name, shape, dt))

            bn0 = mb("bn0", [P, CH, 6])
            st0 = mb("st0", [P, CH, 2])
            ve0 = mb("ve0", [P, CH])
            rs0 = mb("rs0", [P, CH])
            wq_p = mb("wq_p", [P, D])
            wk_p = mb("wk_p", [P, D])
            h0 = mb("h0", [P, CH, D])
            h0T = mb("h0T", [P, W])
            sqa = mb("sqa", [P, W])
            sqb = mb("sqb", [P, W])
            sqs = mb("sqs", [P, W])
            eqk = mb("eqk", [P, W])
            vb = mb("vb", [P, W])
            ov = mb("ov", [P, W])
            bn1 = mb("bn1", [P, CH, 6])
            st1 = mb("st1", [P, CH, 2])
            r1 = mb("r1", [P, CH])
            ve1 = mb("ve1", [P, CH])
            r1sq = mb("r1sq", [P, CH])
            v2 = mb("v2", [P, CH])
            ve2 = mb("ve2", [P, CH])
            r2 = mb("r2", [P, CH])
            rr = mb("rr", [P, CH])
            hh = mb("hh", [P, CH, D])
            hT = mb("hT", [P, W])
            qp = mb("qp", [P, 3, W], bf16)
            kp = mb("kp", [P, 3, W], bf16)
            qr = mb("qr", [P, W])
            kr = mb("kr", [P, W])
            bT0, bAB, bV, bC, bO, bT1, bQK, bV2 = banks

            x_in = [sem(f"x_loaded{b}") for b in range(B)]
            names = ["bn0_done", "st0_done", "eps0_done", "rstd0_done", "h0_done", "h0_turned", "h0T_done",
                     "ab_done", "vproj_done", "sq_done", "sqsum_done", "vb_done", "eqk_done", "coeff_done", "ov_done", "wo_done",
                     "xbo_done", "x1_done", "bn1_done", "st1_done", "eps1_done", "rstd1_done", "r1sq_done",
                     "v2_done", "eps2_done", "r2_done", "rr_done", "hh_done", "hh_turned", "hT_done", "qk_done",
                     "v_done", "part1_done", "rest_done", "part2_done", "part3_done", "vs_done",
                     "qparts_stored", "kparts_stored", "order_done", "stats_kept", "rstd_kept"]
            s = {n: sem(n) for n in names}

            def stages(i, fs):
                for k in reversed(range(len(fs))):
                    if isinstance(i, int) and not 0 <= i - k < NC:
                        continue
                    fs[k](i - k)

            def skewed(eng, fs, before_loop=None):
                lag = len(fs) - 1
                for i in range(lag):
                    stages(i, fs)
                if before_loop:
                    before_loop()
                with eng.Fori(lag, NC) as i:
                    stages(i, fs)
                for i in range(NC, NC + lag):
                    stages(i, fs)

            def first(i):
                return isinstance(i, int) and i == 0

            @block.sync
            def _(sp):
                xv = x.rearrange("b (t p) d -> b p t d", p=P)
                sp.dma_start(xs[:, 0:TB, :], xv[0]).then_inc(x_in[0], 16)
                for dst, src in ((Wq_s, Wq), (Wk_s, Wk), (Wv_s, Wv), (Wo_s, Wo),
                                 (wq_s, wq), (wk_s, wk), (wv_s, wv), (wo_s, wo)):
                    sp.dma_start(dst[:, :], src).then_inc(w_in, 16)
                for dst, src in ((bq_c, bq), (bk_c, bk), (bv_c, bv), (s1_c, ln1_scale), (t1_c, ln1_shift),
                                 (s2_c, ln2_scale), (t2_c, ln2_shift)):
                    sp.dma_start(dst, src.rearrange("(p a) -> p a", a=1)).then_inc(w_in, 16)
                for dst, src in ((bo_r, bo), (fbo_r, fbo)):
                    sp.dma_start(dst[:, :], src.partition_broadcast(P)).then_inc(w_in, 16)
                for b in range(1, B):
                    sp.dma_start(xs[:, b * TB:(b + 1) * TB, :], xv[b]).then_inc(x_in[b], 16)
                qd = qparts.rearrange("h b g a d (i t) -> h b a g (d i) t", i=HG)
                kd = kparts.rearrange("h b g a d (i t) -> h b a g (d i) t", i=HG)
                HC = Q // W
                with sp.Fori(0, NC) as i:
                    wait_alone(sp, s["part3_done"], 2 * i + 2)
                    for parts, dst, stored in ((qp, qd, s["qparts_stored"]), (kp, kd, s["kparts_stored"])):
                        for a in range(3):
                            sp.dma_start(dst[i // HC % 2, i // (2 * HC), a, :, :, bass.ds(i % HC * W, W)], parts[:, a, :])\
                                .then_inc(stored, 16)
                sp.wait_ge(s["qparts_stored"], 48 * NC)
                sp.wait_ge(s["kparts_stored"], 48 * NC)

            @block.gpsimd
            def _(pool):
                g = nc.gpsimd
                g.memset(power[:, :], -0.5).then_inc(consts, 1)
                g.memset(ident[:, :], 0.0).then_inc(consts, 1)
                g.memset(headones[:, :], 1.0).then_inc(consts, 1)
                g.memset(maskb[:, :], 0.0).then_inc(consts, 1)
                pool.wait_ge(consts, 4)
                g.affine_select(out=ident[:, :], in_=ident[:, :], compare_op=ALU.not_equal, fill=1.0,
                                base=0, pattern=[[-1, P]], channel_multiplier=1).then_inc(consts, 1)
                hv = headones[:, :].rearrange("p (h d) -> p h d", d=HD)
                g.affine_select(out=hv, in_=hv, compare_op=ALU.is_ge, fill=0.0, base=0,
                                pattern=[[-HD, H], [0, HD]], channel_multiplier=1).then_inc(consts, 1)
                g.affine_select(out=maskb[:, :], in_=maskb[:, :], compare_op=ALU.is_ge, fill=MASKED,
                                base=0, pattern=[[-1, P]], channel_multiplier=1).then_inc(consts, 1)
                pool.wait_ge(consts, 7)
                g.affine_select(out=hv, in_=hv, compare_op=ALU.is_ge, fill=0.0, base=HD - 1,
                                pattern=[[HD, H], [0, HD]], channel_multiplier=-1).then_inc(consts, 1)
                g.tensor_copy(identb[:, :], ident[:, :]).then_inc(consts, 1)
                pool.wait_ge(w_in, 16 * 17)

                def rsqrt_x(i):
                    wait_alone(pool, s["st0_done"], CH * (i + 1))
                    g.tensor_scalar(ve0[:, :], st0[:, :, 1], EPS, None, ALU.add).then_inc(s["eps0_done"], 1)
                    wait_alone(pool, s["eps0_done"], i + 1)
                    if not first(i):
                        wait_alone(pool, s["h0_done"], CH * i)
                    g.tensor_tensor(rs0[:, :], ve0[:, :], power[:, :], ALU.pow).then_inc(s["rstd0_done"], 1)

                def none(i):
                    pass

                def add_bias_and_rsqrts(i):
                    wait_alone(pool, s["h0_done"], CH * (i + 1))
                    for t in range(CH):
                        g.tensor_tensor(xs[:, CH * i + t, :], xs[:, CH * i + t, :], bo_r[:, :],
                                        ALU.add).then_inc(s["xbo_done"], 1)
                    var = st1[:, :, 1]
                    wait_alone(pool, s["st1_done"], CH * (i + 1))
                    g.tensor_scalar(ve1[:, :], var, EPS, None, ALU.add).then_inc(s["eps1_done"], 1)
                    wait_alone(pool, s["eps1_done"], i + 1)
                    g.tensor_tensor(r1[:, :], ve1[:, :], power[:, :], ALU.pow).then_inc(s["rstd1_done"], 1)
                    wait_alone(pool, s["rstd1_done"], i + 1)
                    g.tensor_tensor(r1sq[:, :], r1[:, :], r1[:, :], ALU.mult).then_inc(s["r1sq_done"], 1)
                    wait_alone(pool, s["r1sq_done"], i + 1)
                    g.tensor_tensor(v2[:, :], r1sq[:, :], var, ALU.mult).then_inc(s["v2_done"], 1)
                    wait_alone(pool, s["v2_done"], i + 1)
                    g.tensor_scalar(ve2[:, :], v2[:, :], EPS, None, ALU.add).then_inc(s["eps2_done"], 1)
                    wait_alone(pool, s["eps2_done"], i + 1)
                    g.tensor_tensor(r2[:, :], ve2[:, :], power[:, :], ALU.pow).then_inc(s["r2_done"], 1)
                    wait_alone(pool, s["r2_done"], i + 1)
                    if not first(i):
                        wait_alone(pool, s["hh_done"], CH * i)
                    g.tensor_tensor(rr[:, :], r1[:, :], r2[:, :], ALU.mult).then_inc(s["rr_done"], 1)
                    g.tensor_copy(stats1[:, bass.ds(CH * i, CH), :], st1[:, :, :]).then_inc(s["stats_kept"], 1)
                    g.tensor_copy(rstd1[:, bass.ds(CH * i, CH)], r1[:, :]).then_inc(s["rstd_kept"], 1)

                def split(i):
                    for n, (parts, rest) in enumerate(((qp, qr), (kp, kr))):
                        wait_alone(pool, s["rest_done"], 2 * i + n + 1)
                        g.tensor_copy(parts[:, 1, :], rest[:, :]).then_inc(s["part2_done"], 1)
                    for n, (parts, rest) in enumerate(((qp, qr), (kp, kr))):
                        wait_alone(pool, s["part2_done"], 2 * i + n + 1)
                        g.tensor_tensor(parts[:, 2, :], rest[:, :], parts[:, 1, :],
                                        ALU.subtract).then_inc(s["part3_done"], 1)
                skewed(pool, [rsqrt_x, none, add_bias_and_rsqrts, split])

            @block.vector
            def _(dve):
                v = nc.vector

                def norm_x(i):
                    if isinstance(i, int):
                        dve.wait_ge(x_in[i * CH // TB], 16)
                    if not first(i):
                        wait_alone(dve, s["eps0_done"], i)
                    for t in range(CH):
                        v.bn_stats(bn0[:, t, :], xs[:, CH * i + t, :]).then_inc(s["bn0_done"], 1)
                    for t in range(CH):
                        wait_alone(dve, s["bn0_done"], CH * i + t + 1)
                        v.bn_aggr(st0[:, t, :], bn0[:, t, :]).then_inc(s["st0_done"], 1)
                    dve.wait_ge(s["rstd0_done"], i + 1)
                    if not first(i):
                        dve.wait_ge(s["h0_turned"], i)
                    for t in range(CH):
                        v.tensor_scalar(h0[:, t, :], xs[:, CH * i + t, :], st0[:, t, 0:1], rs0[:, t:t + 1],
                                        ALU.subtract, ALU.mult).then_inc(s["h0_done"], 1)

                def square_sum(i):
                    dve.wait_ge(s["sq_done"], 2 * i + 2)
                    if not first(i):
                        dve.wait_ge(s["eqk_done"], i)
                    v.tensor_tensor(sqs[:, :], sqa[:, :], sqb[:, :], ALU.add).then_inc(s["sqsum_done"], 1)

                def mix_and_norm(i):
                    dve.wait_ge(s["coeff_done"], i + 1)
                    dve.wait_ge(s["vb_done"], i + 1)
                    if not first(i):
                        dve.wait_ge(s["wo_done"], i)
                    v.tensor_tensor(ov[:, :], bC[:, 0:W], vb[:, :], ALU.mult).then_inc(s["ov_done"], 1)
                    dve.wait_ge(s["wo_done"], i + 1)
                    dve.wait_ge(s["xbo_done"], CH * (i + 1))
                    x1 = xs[:, bass.ds(CH * i, CH), :]
                    v.tensor_tensor(x1, bO[:, 0:W].rearrange("p (t d) -> p t d", t=CH), x1,
                                    ALU.add).then_inc(s["x1_done"], 1)
                    wait_alone(dve, s["x1_done"], i + 1)
                    for t in range(CH):
                        v.bn_stats(bn1[:, t, :], xs[:, CH * i + t, :]).then_inc(s["bn1_done"], 1)
                    if not first(i):
                        wait_alone(dve, s["stats_kept"], i)
                    for t in range(CH):
                        wait_alone(dve, s["bn1_done"], CH * i + t + 1)
                        v.bn_aggr(st1[:, t, :], bn1[:, t, :]).then_inc(s["st1_done"], 1)
                    dve.wait_ge(s["rr_done"], i + 1)
                    if not first(i):
                        dve.wait_ge(s["hh_turned"], i)
                    for t in range(CH):
                        v.tensor_scalar(hh[:, t, :], xs[:, CH * i + t, :], st1[:, t, 0:1],
                                        rr[:, t:t + 1], ALU.subtract, ALU.mult).then_inc(s["hh_done"], 1)

                def rests(i):
                    for n, (parts, rest) in enumerate(((qp, qr), (kp, kr))):
                        dve.wait_ge(s["part1_done"], 2 * i + 2)
                        if not first(i):
                            dve.wait_ge(s["part3_done"], 2 * i)
                        v.tensor_tensor(rest[:, :], bQK[:, n * W:(n + 1) * W], parts[:, 0, :],
                                        ALU.subtract).then_inc(s["rest_done"], 1)

                def all_loaded():
                    for b in range(B):
                        dve.wait_ge(x_in[b], 16)
                skewed(dve, [norm_x, square_sum, mix_and_norm, rests], all_loaded)

            @block.scalar
            def _(act):
                a = nc.scalar
                act.wait_ge(w_in, 16 * 17)
                for dst, src in ((wq_p, wq_s), (wk_p, wk_s)):
                    a.copy(dst[:, :].rearrange("p (g d i) -> p g d i", d=HD, i=HG),
                           src[:, :].rearrange("p (g i d) -> p g d i", d=HD, i=HG)).then_inc(s["order_done"], 1)

                def none(i):
                    pass

                def project(i):
                    act.wait_ge(s["h0_turned"], i + 1)
                    if not first(i):
                        act.wait_ge(s["vproj_done"], i)
                    a.copy(h0T[:, :], bT0[:, 0:W]).then_inc(s["h0T_done"], 1)
                    act.wait_ge(s["ab_done"], i + 1)
                    if not first(i):
                        act.wait_ge(s["sqsum_done"], i)
                    a.activation(sqa[:, :], bAB[:, 0:W], ACT.Square, bias=bq_c).then_inc(s["sq_done"], 1)
                    a.activation(sqb[:, :], bAB[:, W:2 * W], ACT.Square, bias=bk_c).then_inc(s["sq_done"], 1)
                    act.wait_ge(s["vproj_done"], i + 1)
                    if not first(i):
                        act.wait_ge(s["ov_done"], i)
                    a.activation(vb[:, :], bV[:, 0:W], ACT.Identity, bias=bv_c).then_inc(s["vb_done"], 1)
                    act.wait_ge(s["sqsum_done"], i + 1)
                    if not first(i):
                        act.wait_ge(s["coeff_done"], i)
                    a.activation(eqk[:, :], sqs[:, :], ACT.Exp, scale=-0.5).then_inc(s["eqk_done"], 1)

                def heads(i):
                    act.wait_ge(s["hh_turned"], i + 1)
                    if not first(i):
                        act.wait_ge(s["v_done"], i)
                    a.activation(hT[:, :], bT1[:, 0:W], ACT.Identity, bias=t1_c, scale=s1_c).then_inc(s["hT_done"], 1)
                    act.wait_ge(s["qk_done"], i + 1)
                    if not first(i):
                        act.wait_ge(s["qparts_stored"], 48 * i)
                    a.copy(qp[:, 0, :], bQK[:, 0:W]).then_inc(s["part1_done"], 1)
                    if not first(i):
                        act.wait_ge(s["kparts_stored"], 48 * i)
                    a.copy(kp[:, 0, :], bQK[:, W:2 * W]).then_inc(s["part1_done"], 1)
                    act.wait_ge(s["v_done"], i + 1)
                    a.copy(vs[:, bass.ds(CH * i, CH), :], bV2[:, 0:W].rearrange("p (t d) -> p t d", t=CH))\
                        .then_inc(s["vs_done"], 1)
                skewed(act, [none, project, none, heads])

            @block.tensor
            def _(pe):
                t_ = nc.tensor
                pe.wait_ge(consts, 9)
                pe.wait_ge(w_in, 16 * 17)
                pe.wait_ge(s["order_done"], 2)

                def none(i):
                    pass

                def project(i):
                    pe.wait_ge(s["h0_done"], CH * (i + 1))
                    if not first(i):
                        pe.wait_ge(s["h0T_done"], i)
                    for t in range(CH):
                        last = t_.transpose(bT0[:, t * P:(t + 1) * P], h0[:, t, :], ident[:, :])
                    last.then_inc(s["h0_turned"], 1)
                    pe.wait_ge(s["h0T_done"], i + 1)
                    if not first(i):
                        pe.wait_ge(s["sq_done"], 2 * i)
                    t_.matmul(bAB[:, 0:W], Wq_s[:, :], h0T[:, :], start=True, stop=True)
                    t_.matmul(bAB[:, W:2 * W], Wk_s[:, :], h0T[:, :], start=True, stop=True).then_inc(s["ab_done"], 1)
                    if not first(i):
                        pe.wait_ge(s["vb_done"], i)
                    t_.matmul(bV[:, 0:W], Wv_s[:, :], h0T[:, :], start=True, stop=True).then_inc(s["vproj_done"], 1)

                def mix_out(i):
                    pe.wait_ge(s["eqk_done"], i + 1)
                    if not first(i):
                        pe.wait_ge(s["ov_done"], i)
                    t_.matmul(bC[:, 0:W], headones[:, :], eqk[:, :], start=True, stop=True).then_inc(s["coeff_done"], 1)
                    pe.wait_ge(s["ov_done"], i + 1)
                    if not first(i):
                        pe.wait_ge(s["x1_done"], i)
                    for t in range(CH):
                        last = t_.matmul(bO[:, t * P:(t + 1) * P], ov[:, t * P:(t + 1) * P], Wo_s[:, :],
                                         start=True, stop=True)
                    last.then_inc(s["wo_done"], 1)

                def heads(i):
                    pe.wait_ge(s["hh_done"], CH * (i + 1))
                    if not first(i):
                        pe.wait_ge(s["hT_done"], i)
                    for t in range(CH):
                        last = t_.transpose(bT1[:, t * P:(t + 1) * P], hh[:, t, :], ident[:, :])
                    last.then_inc(s["hh_turned"], 1)
                    pe.wait_ge(s["hT_done"], i + 1)
                    if not first(i):
                        pe.wait_ge(s["rest_done"], 2 * i)
                    t_.matmul(bQK[:, 0:W], wq_p[:, :], hT[:, :], start=True, stop=True)
                    t_.matmul(bQK[:, W:2 * W], wk_p[:, :], hT[:, :], start=True, stop=True).then_inc(s["qk_done"], 1)
                    if not first(i):
                        pe.wait_ge(s["vs_done"], i)
                    for t in range(CH):
                        last = t_.matmul(bV2[:, t * P:(t + 1) * P], hT[:, t * P:(t + 1) * P], wv_s[:, :],
                                         start=True, stop=True)
                    last.then_inc(s["v_done"], 1)
                skewed(pe, [none, project, mix_out, heads])

        with ExitStack() as at, nc.Block() as block:
            def ab(name, shape, dt=fp32):
                return at.enter_context(nc.sbuf_tensor(name, shape, dt))

            NS = 2
            qop = [ab(f"qop{i}", [P, HG, S], bf16) for i in range(NS)]
            kop = [ab(f"kop{i}", [P, HG, S], bf16) for i in range(NS)]
            vop = [ab(f"vop{i}", [P, TB, HG, 32]) for i in range(NS)]
            NP = 4
            probs = [ab(f"probs{i}", [P, HG, Q]) for i in range(NP)]
            negmax = ab("negmax", [P, HG, TB])
            negmax1 = ab("negmax1", [P, HG, TB // 2])
            negparts = ab("negparts", [P, 2, HG, TB], bf16)
            negrows = ab("negrows", [2 * HG * TB, P], bf16)
            ctxT = ab("ctxT", [P, Q])
            recip = ab("recip", [P, 4, HG])
            expb, maxb, pvb, miscb = banks[0:3], banks[3:6], banks[6], banks[7]

            late_in = [sem(f"late_operands_loaded{i}") for i in range(NS)]
            early_in = [sem(f"early_operands_loaded{i}") for i in range(NS)]
            rows_in = [sem(f"maxrows_loaded{i}") for i in range(NS)]
            names = ["operands_cleared", "operands_ones", "st_done", "exp_done", "select_done", "vop_ready", "pv_done",
                     "ctx_out", "ctx_turned", "recip_done", "ctx_done", "max_done", "maxred_done", "negmax_done",
                     "neghi_done", "neglo_done", "neg_turned", "neg_out"]
            s = {n: sem(n) for n in names}
            CLEARS = 2 * NS

            def turns(eng, body):
                body(0, 0, 0)
                with eng.Fori(0, NG // 2 - 1) as p:
                    body(2 * p + 1, p, 1)
                    body(2 * p + 2, p + 1, 0)
                body(NG - 1, NG // 2 - 1, 1)

            def is_first(g):
                return isinstance(g, int) and g == 0

            def is_last(g):
                return isinstance(g, int) and g == NG - 1

            def nxt(g, k, par):
                return g + 1, (k if par < NS - 1 else k + 1), (par + 1) % NS

            @block.sync
            def _(sp):
                def load(g, par, half):
                    toks = slice(half * Q, (half + 1) * Q)
                    loaded = (late_in if half else early_in)[par]
                    row = 0
                    for part, times in ((0, 3), (1, 2), (2, 1)):
                        src = qparts[half, g // 4, g % 4, part].unsqueeze(0).to_broadcast([times, HD, HG * Q])
                        sp.dma_start(qop[par][row:row + times * HD, :, toks], src).then_inc(loaded, 16)
                        sp.dma_start(kop[par][row:row + times * HD, :, toks],
                                     kparts[half, g // 4, g % 4, 0:times].rearrange("a d t -> (a d) t"))\
                            .then_inc(loaded, 16)
                        row += times * HD

                def max_rows(g, k, par):
                    sp.wait_ge(s["neg_out"], g + 1)
                    for n in range(2):
                        sp.dma_start(qop[par][KS + n:KS + n + 1, :, :].rearrange("p i (t q) -> p (i t) q", q=P),
                                     negrows[n * HG * TB:(n + 1) * HG * TB, :]).then_inc(rows_in[par], 16)
                sp.wait_ge(s["operands_cleared"], CLEARS)
                for g in range(NS):
                    load(g, g, 1)
                    load(g, g, 0)
                max_rows(0, 0, 0)

                def turn(g, k, par):
                    more = not (isinstance(g, int) and g + 2 >= NG)
                    if more:
                        wait_alone(sp, s["st_done"], NEU * g + LATE_UNITS)
                        load(g + 2, par, 1)
                    if not is_last(g):
                        max_rows(*nxt(g, k, par))
                    if more:
                        wait_alone(sp, s["st_done"], NEU * (g + 1))
                        load(g + 2, par, 0)
                turn(0, 0, 0)
                with sp.Fori(0, NG // 2 - 2) as p:
                    turn(2 * p + 1, p, 1)
                    turn(2 * p + 2, p + 1, 0)
                for g in range(NG - 3, NG):
                    turn(g, g // 2, g % 2)

            @block.gpsimd
            def _(pool):
                g_ = nc.gpsimd
                for i in range(NS):
                    g_.memset(qop[i][:, :, :], 0.0).then_inc(s["operands_cleared"], 1)
                    g_.memset(vop[i][:, :, :, :], 0.0).then_inc(s["operands_ones"], 1)
                pool.wait_ge(s["operands_cleared"], CLEARS)
                pool.wait_ge(s["operands_ones"], NS)
                for i in range(NS):
                    g_.memset(kop[i][KS:KM, :, :], 1.0).then_inc(s["operands_ones"], 1)
                wait_alone(pool, s["operands_ones"], 2 * NS)
                for i in range(NS):
                    g_.memset(vop[i][:, :, :, HD:HD + 1], 1.0).then_inc(s["operands_ones"], 1)

                def vcopy(g, k, par):
                    if not (isinstance(g, int) and g < 2):
                        wait_alone(pool, s["pv_done"], NEG * (g - 1))
                    src = vs[:, bass.ds((g // 4) * TB, TB), bass.ds((g % 4) * HG * HD, HG * HD)]
                    g_.tensor_copy(vop[par][:, :, :, 0:HD], src.rearrange("p t (i d) -> p t i d", d=HD))\
                        .then_inc(s["vop_ready"], 1)
                wait_alone(pool, s["operands_ones"], 3 * NS)
                vcopy(0, 0, 0)

                def turn(g, k, par):
                    for n in range(NEG):
                        if EXPG[n][3]:
                            wait_alone(pool, s["exp_done"], NEU * g + UNITS_UNTIL[n])
                            d = probs[n % NP][:, :, 0:P]
                            g_.affine_select(out=d, in_=d, compare_op=ALU.is_ge, fill=0.0, base=0,
                                             pattern=[[0, HG], [1, P]], channel_multiplier=-1)\
                                .then_inc(s["select_done"], 1)
                        if n == 6 and not is_last(g):
                            vcopy(*nxt(g, k, par))
                turns(pool, turn)

            @block.vector
            def _(dve):
                v = nc.vector
                for i in range(NS):
                    v.memset(kop[i][:, :, :], 0.0).then_inc(s["operands_cleared"], 1)

                def max_unit(g, m):
                    t, c, i, n, w = MAXU[m]
                    dve.wait_ge(s["max_done"], NMU * g + m + 1)
                    dst = negmax[:, i:i + n, t:t + 1] if c == 0 else negmax1[:, i:i + n, t - 4:t - 3]
                    src = maxb[MAXB[m]][:, 0:n * w].rearrange("p (i k) -> p i k", i=n)
                    v.tensor_reduce(dst, src, X, ALU.max, negate=True).then_inc(s["maxred_done"], 1)

                def row_max(g):
                    dve.wait_ge(s["maxred_done"], NMU * (g + 1))
                    late = negmax[:, :, TB // 2:TB]
                    v.tensor_tensor(late, late, negmax1[:, :, :], ALU.min).then_inc(s["negmax_done"], 1)
                    dve.wait_ge(s["negmax_done"], g + 1)
                    if not is_first(g):
                        dve.wait_ge(s["neg_turned"], g)
                    v.tensor_copy(negparts[:, 0, :, :], negmax[:, :, :]).then_inc(s["neghi_done"], 1)
                    dve.wait_ge(s["neghi_done"], g + 1)
                    v.tensor_tensor(negparts[:, 1, :, :], negmax[:, :, :], negparts[:, 0, :, :], ALU.subtract)\
                        .then_inc(s["neglo_done"], 1)

                def max_rows_out(g):
                    dve.wait_ge(s["neg_turned"], g + 1)
                    if not is_first(g):
                        dve.wait_ge(*rows_before(g))
                    v.tensor_copy(negrows[:, :], miscb[0:2 * HG * TB, 0:P // 2].bitcast(bf16))\
                        .then_inc(s["neg_out"], 1)

                par_of = {}

                def rows_before(g):
                    par, k = par_of["now"]
                    return rows_in[(par - 1) % NS], 32 * (k if par == 0 else k + 1)

                def normalize(g, half):
                    dve.wait_ge(s["ctx_turned"], 2 * g + half + 1)
                    cv = miscb[:, :].rearrange("p (t i c) -> p t i c", t=4, i=HG)
                    v.reciprocal(recip[:, :, :], cv[:, :, :, HD]).then_inc(s["recip_done"], 1)
                    dve.wait_ge(s["recip_done"], 2 * g + half + 1)
                    first_tile = (g // 4) * TB + (4 if half == 0 else 0)
                    dst = att[:, bass.ds(first_tile, 4), bass.ds((g % 4) * HG * HD, HG * HD)]
                    v.tensor_tensor(dst.rearrange("p t (i d) -> p t i d", d=HD), cv[:, :, :, 0:HD],
                                    recip[:, :, :].unsqueeze(3).to_broadcast([P, 4, HG, HD]), ALU.mult)\
                        .then_inc(s["ctx_done"], 1)

                par_of["now"] = (0, 0)
                for m in range(NMU):
                    max_unit(0, m)
                row_max(0)
                max_rows_out(0)

                def turn(g, k, par):
                    for what, m in TURN:
                        if what == "max" and not is_last(g):
                            max_unit(g + 1, m)
                        if what == "negate_max" and not is_last(g):
                            row_max(g + 1)
                        if what == "turn_max" and not is_last(g):
                            g1, k1, par1 = nxt(g, k, par)
                            par_of["now"] = (par1, k1)
                            max_rows_out(g1)
                        if what == "turn_ctx" and m == 1 and not is_first(g):
                            normalize(g - 1, 1)
                        if what == "turn_ctx" and m == 0:
                            normalize(g, 0)
                turns(dve, turn)
                normalize(NG - 1, 1)

            @block.scalar
            def _(act):
                a = nc.scalar

                def exp_unit(g, e):
                    n, i, heads = EXPU[e]
                    w = EXPG[n][2]
                    if i == 0 and not (is_first(g) and n < NP):
                        act.wait_ge(s["pv_done"], NEG * g + n - NP + 1)
                    act.wait_ge(s["st_done"], NEU * g + e + 1)
                    a.activation(probs[n % NP][:, i:i + heads, 0:w],
                                 expb[EXPB[e]][:, 0:heads * w].rearrange("p (i q) -> p i q", i=heads),
                                 ACT.Exp, scale=SCALE).then_inc(s["exp_done"], 1)

                def ctx_copy(g, half):
                    act.wait_ge(s["pv_done"], NEG * g + (8 if half == 0 else 12))
                    if not (is_first(g) and half == 0):
                        act.wait_ge(s["ctx_turned"], 2 * g + half)
                    a.copy(ctxT[:, :], pvb[:, :]).then_inc(s["ctx_out"], 1)

                def turn(g, k, par):
                    for what, m in TURN:
                        if what == "exp":
                            exp_unit(g, m)
                        if what == "copy_ctx" and m == 1 and not is_first(g):
                            ctx_copy(g - 1, 1)
                        if what == "copy_ctx" and m == 0:
                            ctx_copy(g, 0)
                turns(act, turn)
                ctx_copy(NG - 1, 1)

            @block.tensor
            def _(pe):
                t_ = nc.tensor

                def max_unit(g, k, par, m):
                    t, c, i, n, w = MAXU[m]
                    if m == 0:
                        pe.wait_ge(late_in[par], LOADS * (k + 1))
                    if m == LATE_KEYS:
                        pe.wait_ge(early_in[par], LOADS * (k + 1))
                    if not (is_first(g) and m < 3):
                        pe.wait_ge(s["maxred_done"], NMU * g + since(MAXB, m))
                    diag = c == 1 or t < 4
                    for h in range(n):
                        o = maxb[MAXB[m]][:, h * w:(h + 1) * w]
                        last = t_.matmul(o, qop[par][0:KS, i + h, t * P:(t + 1) * P],
                                         kop[par][0:KS, i + h, c * Q:c * Q + w], start=True, stop=not diag)
                        if diag:
                            last = t_.matmul(o[:, w - P:w], identb[:, :], maskb[:, :], start=False, stop=True)
                    last.then_inc(s["max_done"], 1)

                def st_unit(g, par, e):
                    n, i, heads = EXPU[e]
                    c, j, w, _ = EXPG[n]
                    if not (is_first(g) and e < 3):
                        pe.wait_ge(s["exp_done"], NEU * g + since(EXPB, e))
                    q0 = max(c * Q, j * P)
                    for h in range(heads):
                        last = t_.matmul(expb[EXPB[e]][:, h * w:(h + 1) * w], kop[par][0:KM, i + h, j * P:(j + 1) * P],
                                         qop[par][0:KM, i + h, q0:q0 + w], start=True, stop=True)
                    last.then_inc(s["st_done"], 1)

                def pv_group(g, par, n):
                    c, j, w, diag = EXPG[n]
                    if n == 0:
                        pe.wait_ge(s["vop_ready"], g + 1)
                        if not is_first(g):
                            pe.wait_ge(s["ctx_out"], 2 * g)
                    if n == 8:
                        pe.wait_ge(s["ctx_out"], 2 * g + 1)
                    pe.wait_ge(s["exp_done"], NEU * g + UNITS_UNTIL[n])
                    if diag:
                        pe.wait_ge(s["select_done"], NDG * g + DIAG_UNTIL[n])
                    for i in range(HG):
                        last = t_.matmul(pvb[32 * i:32 * i + 32, Q - w:Q], vop[par][:, j, i, :],
                                         probs[n % NP][:, i, 0:w], start=j == 0, stop=j == 4 * c + 3)
                    last.then_inc(s["pv_done"], 1)

                def turn_ctx(g, half):
                    pe.wait_ge(s["ctx_out"], 2 * g + half + 1)
                    if half == 1:
                        pe.wait_ge(s["ctx_done"], 2 * g + 1)
                    elif is_last(g):
                        pe.wait_ge(s["ctx_done"], 2 * g)
                    else:
                        pe.wait_ge(s["neg_out"], g + 2)
                    for t in range(4):
                        last = t_.transpose(miscb[:, t * P:(t + 1) * P], ctxT[:, t * P:(t + 1) * P], ident[:, :])
                    last.then_inc(s["ctx_turned"], 1)

                def turn_max(g):
                    wait_alone(pe, s["neglo_done"], g + 1)
                    if isinstance(g, int) and g == 1:
                        pe.wait_ge(s["neg_out"], 1)
                    elif not is_first(g):
                        wait_alone(pe, s["ctx_done"], 2 * g - 2)
                    t_.transpose(miscb[0:2 * HG * TB, 0:P // 2].bitcast(bf16),
                                 negparts[:, :, :, :].rearrange("p a i t -> p (a i t)"), identb[:, :])\
                        .then_inc(s["neg_turned"], 1)

                LOADS = 2 * 3 * 16
                pe.wait_ge(s["operands_ones"], 3 * NS)
                for m in range(NMU):
                    max_unit(0, 0, 0, m)
                turn_max(0)

                def turn(g, k, par):
                    g1, k1, par1 = nxt(g, k, par)
                    pe.wait_ge(rows_in[par], 32 * (k + 1))
                    for what, m in TURN:
                        if what == "exp":
                            st_unit(g, par, m)
                        if what == "max" and not is_last(g):
                            max_unit(g1, k1, par1, m)
                        if what == "pv" and m >= 0:
                            pv_group(g, par, m)
                        if what == "pv" and m < 0 and not is_first(g):
                            pv_group(g - 1, (par - 1) % NS, NEG + m)
                        if what == "turn_ctx" and m == 1 and not is_first(g):
                            turn_ctx(g - 1, 1)
                        if what == "turn_ctx" and m == 0:
                            turn_ctx(g, 0)
                        if what == "turn_max" and not is_last(g):
                            turn_max(g1)
                turns(pe, turn)
                for n in range(NEG - PV_LAG, NEG):
                    pv_group(NG - 1, (NG - 1) % NS, n)
                turn_ctx(NG - 1, 1)

        h2T = sb("h2T", [P, NT * P])
        logits = sb("logits", [P, NT, EX])
        gate_s = sb("gate_s", [P, EX])
        w1_s = sb("w1_s", [P, EX, HID])
        w2_s = sb("w2_s", [P, EX, HID])
        w3_s = sb("w3_s", [P, EX, HID // P, D])
        wts = sb("wts", [P, NT, EX])
        ffn_in = sem("ffn_weights_loaded")

        with ExitStack() as fi, nc.Block() as block:
            def fb(name, shape, dt=fp32):
                return fi.enter_context(nc.sbuf_tensor(name, shape, dt))

            attc = fb("attc", [P, CH, D])
            attT = fb("attT", [P, W])
            hzT = fb("hzT", [P, W])
            yb = fb("yb", [P, CH, D])
            z = fb("z", [P, CH, D])
            bn2 = fb("bn2", [P, CH, 6])
            st2 = fb("st2", [P, CH, 2])
            ve3 = fb("ve3", [P, CH])
            rs2 = fb("rs2", [P, CH])
            hz = fb("hz", [P, CH, D])
            rank = fb("rank", [P, EX])
            sel = fb("sel", [P, NT, EX])
            oh1 = fb("oh1", [P, NT, EX])
            oh2 = fb("oh2", [P, NT, EX])
            rest = fb("rest", [P, NT, EX])
            best = fb("best", [P, 2, NT])
            pick = fb("pick", [P, NT])
            gap = fb("gap", [P, NT])
            egap = fb("egap", [P, NT])
            eone = fb("eone", [P, NT])
            pr = fb("pr", [P, 2, NT])
            bA, bZ, bH, bG = banks[0:4]
            names = ["attc_done", "hzT_done", "att_turned", "attT_done", "wo2_done", "y_done", "yb_done", "z_done", "resid_done", "bn2_done",
                     "st2_done", "eps3_done", "rs2_done", "hz_done", "hz_turned", "h2T_done", "gate_done",
                     "logits_done", "rank_done", "gap_done", "egap_done", "gating_step"]
            s = {n: sem(n) for n in names}

            def stages(i, fs):
                for k in reversed(range(len(fs))):
                    if isinstance(i, int) and not 0 <= i - k < NC:
                        continue
                    fs[k](i - k)

            def skewed(eng, fs):
                lag = len(fs) - 1
                for i in range(lag):
                    stages(i, fs)
                with eng.Fori(lag, NC) as i:
                    stages(i, fs)
                for i in range(NC, NC + lag):
                    stages(i, fs)

            def first(i):
                return isinstance(i, int) and i == 0

            def none(i):
                pass

            @block.sync
            def _(sp):
                sp.dma_start(gate_s[:, :], gate_w).then_inc(ffn_in, 16)
                sp.dma_start(w1_s[:, :, :], w1.rearrange("e d h -> d e h")).then_inc(ffn_in, 16)
                sp.dma_start(w2_s[:, :, :], w2.rearrange("e d h -> d e h")).then_inc(ffn_in, 16)
                for k in range(HID // P):
                    sp.dma_start(w3_s[:, :, k, :], w3[:, k * P:(k + 1) * P, :].rearrange("e h d -> h e d"))\
                        .then_inc(ffn_in, 16)

            @block.gpsimd
            def _(pool):
                g = nc.gpsimd
                for e in range(EX):
                    last = g.memset(rank[:, e:e + 1], float(EX - e))
                last.then_inc(s["rank_done"], 1)

                def make_z(i):
                    wait_alone(pool, s["y_done"], CH * (i + 1))
                    for t in range(CH):
                        g.tensor_tensor(yb[:, t, :], yb[:, t, :], fbo_r[:, :], ALU.add).then_inc(s["yb_done"], 1)
                    wait_alone(pool, s["z_done"], i + 1)
                    xz = xs[:, bass.ds(CH * i, CH), :]
                    g.tensor_tensor(xz, xz, z[:, :, :], ALU.add).then_inc(s["resid_done"], 1)
                    wait_alone(pool, s["st2_done"], CH * (i + 1))
                    g.tensor_scalar(ve3[:, :], st2[:, :, 1], EPS, None, ALU.add).then_inc(s["eps3_done"], 1)
                    wait_alone(pool, s["eps3_done"], i + 1)
                    if not first(i):
                        wait_alone(pool, s["hz_done"], CH * i)
                    g.tensor_tensor(rs2[:, :], ve3[:, :], power[:, :], ALU.pow).then_inc(s["rs2_done"], 1)

                def none(i):
                    pass

                def copy_att(i):
                    if not first(i):
                        wait_alone(pool, s["att_turned"], i)
                    g.tensor_copy(attc[:, :, :], att[:, bass.ds(CH * i, CH), :]).then_inc(s["attc_done"], 1)
                skewed(pool, [copy_att, make_z, none])

            @block.vector
            def _(dve):
                v = nc.vector

                def make_z(i):
                    if not first(i):
                        dve.wait_ge(s["z_done"], i)
                        dve.wait_ge(s["resid_done"], i)
                        dve.wait_ge(s["hz_done"], CH * i)
                    for t in range(CH):
                        v.tensor_scalar(yb[:, t, :], xs[:, CH * i + t, :], stats1[:, CH * i + t, 0:1],
                                        rstd1[:, bass.ds(CH * i + t, 1)], ALU.subtract, ALU.mult)\
                            .then_inc(s["y_done"], 1)
                    dve.wait_ge(s["wo2_done"], i + 1)
                    dve.wait_ge(s["yb_done"], CH * (i + 1))
                    v.tensor_tensor(z[:, :, :], bZ[:, 0:W].rearrange("p (t d) -> p t d", t=CH), yb[:, :, :],
                                    ALU.add).then_inc(s["z_done"], 1)
                    wait_alone(dve, s["z_done"], i + 1)
                    for t in range(CH):
                        v.bn_stats(bn2[:, t, :], z[:, t, :]).then_inc(s["bn2_done"], 1)
                    for t in range(CH):
                        wait_alone(dve, s["bn2_done"], CH * i + t + 1)
                        v.bn_aggr(st2[:, t, :], bn2[:, t, :]).then_inc(s["st2_done"], 1)
                    dve.wait_ge(s["rs2_done"], i + 1)
                    if not first(i):
                        dve.wait_ge(s["hz_turned"], i)
                    for t in range(CH):
                        v.tensor_scalar(hz[:, t, :], z[:, t, :], st2[:, t, 0:1], rs2[:, t:t + 1],
                                        ALU.subtract, ALU.mult).then_inc(s["hz_done"], 1)

                def gate(i):
                    dve.wait_ge(s["gate_done"], i + 1)
                    v.tensor_copy(logits[:, bass.ds(CH * i, CH), :],
                                  bG[:, 0:CH * EX].rearrange("p (t e) -> p t e", e=EX)).then_inc(s["logits_done"], 1)
                skewed(dve, [none, make_z, gate])

                steps = [0]

                def step(ins):
                    steps[0] += 1
                    ins.then_inc(s["gating_step"], 1)
                    dve.wait_ge(s["gating_step"], steps[0])
                rk = rank[:, :].unsqueeze(1).to_broadcast([P, NT, EX])

                def wide(a):
                    return a.unsqueeze(2).to_broadcast([P, NT, EX])

                def choose(scores, m, onehot):
                    step(v.tensor_reduce(best[:, m, :], scores, X, ALU.max))
                    step(v.tensor_tensor(sel[:, :, :], scores, wide(best[:, m, :]), ALU.is_equal))
                    step(v.tensor_tensor(sel[:, :, :], sel[:, :, :], rk, ALU.mult))
                    step(v.tensor_reduce(pick[:, :], sel[:, :, :], X, ALU.max))
                    step(v.tensor_tensor(onehot[:, :, :], rk, wide(pick[:, :]), ALU.is_equal))
                dve.wait_ge(s["logits_done"], NC)
                dve.wait_ge(s["rank_done"], 1)
                choose(logits[:, :, :], 0, oh1)
                step(v.tensor_scalar(sel[:, :, :], oh1[:, :, :], -1.0, 1.0, ALU.mult, ALU.add))
                step(v.tensor_tensor(rest[:, :, :], logits[:, :, :], sel[:, :, :], ALU.mult))
                step(v.tensor_scalar(sel[:, :, :], oh1[:, :, :], MASKED, None, ALU.mult))
                step(v.tensor_tensor(rest[:, :, :], rest[:, :, :], sel[:, :, :], ALU.add))
                choose(rest[:, :, :], 1, oh2)
                v.tensor_tensor(gap[:, :], best[:, 1, :], best[:, 0, :], ALU.subtract).then_inc(s["gap_done"], 1)
                dve.wait_ge(s["egap_done"], 1)
                step(v.tensor_scalar(eone[:, :], egap[:, :], 1.0, None, ALU.add))
                step(v.reciprocal(pr[:, 0, :], eone[:, :]))
                step(v.tensor_tensor(pr[:, 1, :], pr[:, 0, :], egap[:, :], ALU.mult))
                step(v.tensor_tensor(oh1[:, :, :], oh1[:, :, :], wide(pr[:, 0, :]), ALU.mult))
                step(v.tensor_tensor(oh2[:, :, :], oh2[:, :, :], wide(pr[:, 1, :]), ALU.mult))
                step(v.tensor_tensor(wts[:, :, :], oh1[:, :, :], oh2[:, :, :], ALU.add))

            @block.scalar
            def _(act):
                a = nc.scalar

                def att_copy(i):
                    act.wait_ge(s["att_turned"], i + 1)
                    if not first(i):
                        act.wait_ge(s["wo2_done"], i)
                    a.copy(attT[:, :], bA[:, 0:W]).then_inc(s["attT_done"], 1)

                def scale_shift(i):
                    act.wait_ge(s["hz_turned"], i + 1)
                    if not first(i):
                        act.wait_ge(s["gate_done"], i)
                    a.activation(hzT[:, :], bH[:, 0:W], ACT.Identity, bias=t2_c, scale=s2_c).then_inc(s["hzT_done"], 1)
                    act.wait_ge(s["hzT_done"], i + 1)
                    a.copy(h2T[:, bass.ds(i * W, W)], hzT[:, :]).then_inc(s["h2T_done"], 1)
                skewed(act, [none, att_copy, scale_shift])
                act.wait_ge(s["gap_done"], 1)
                a.activation(egap[:, :], gap[:, :], ACT.Exp).then_inc(s["egap_done"], 1)

            @block.tensor
            def _(pe):
                t_ = nc.tensor

                def att_out(i):
                    pe.wait_ge(s["attc_done"], i + 1)
                    if not first(i):
                        pe.wait_ge(s["attT_done"], i)
                    for t in range(CH):
                        last = t_.transpose(bA[:, t * P:(t + 1) * P], attc[:, t, :], ident[:, :])
                    last.then_inc(s["att_turned"], 1)
                    pe.wait_ge(s["attT_done"], i + 1)
                    if not first(i):
                        pe.wait_ge(s["z_done"], i)
                    for t in range(CH):
                        last = t_.matmul(bZ[:, t * P:(t + 1) * P], attT[:, t * P:(t + 1) * P], wo_s[:, :],
                                         start=True, stop=True)
                    last.then_inc(s["wo2_done"], 1)

                def norm_out(i):
                    pe.wait_ge(s["hz_done"], CH * (i + 1))
                    if not first(i):
                        pe.wait_ge(s["hzT_done"], i)
                    for t in range(CH):
                        last = t_.transpose(bH[:, t * P:(t + 1) * P], hz[:, t, :], ident[:, :])
                    last.then_inc(s["hz_turned"], 1)
                    pe.wait_ge(s["hzT_done"], i + 1)
                    if not first(i):
                        pe.wait_ge(s["logits_done"], i)
                    for t in range(CH):
                        last = t_.matmul(bG[:, t * EX:(t + 1) * EX], hzT[:, t * P:(t + 1) * P], gate_s[:, :],
                                         start=True, stop=True)
                    last.then_inc(s["gate_done"], 1)
                pe.wait_ge(ffn_in, 16 * 5)
                skewed(pe, [none, att_out, norm_out])

        with ExitStack() as ff, nc.Block() as block:
            def eb(name, shape, dt=fp32):
                return ff.enter_context(nc.sbuf_tensor(name, shape, dt))

            NCH = NT * P // Q
            TQ = Q // P
            KH = HID // P
            NU = EX * KH
            silu = [eb(f"silu{i}", [P, Q]) for i in range(2)]
            hid = [eb(f"hid{i}", [P, KH, Q]) for i in range(2)]
            wc = eb("wc", [P, TQ, EX])
            base = eb("base", [P, TQ, D])
            acc = eb("acc", [P, TQ, D])
            outb = eb("outb", [P, TQ, D])
            gb, ub, ob = banks[0:3], banks[3:6], banks[6:8]
            UPB = [u % 3 for u in range(NU - 1)] + [1]
            names = ["up_done", "silu_done", "hid_done", "down_done", "acc_done", "chunk_ready", "out_stored"]
            s = {n: sem(n) for n in names}

            def is_first(c):
                return isinstance(c, int) and c == 0

            @block.sync
            def _(sp):
                ov = out.rearrange("b s d -> (b s) d").rearrange("(c t p) d -> c p t d", p=P, t=TQ)
                with sp.Fori(0, NCH) as c:
                    sp.wait_ge(s["acc_done"], EX * TQ * (c + 1))
                    sp.dma_start(ov[c], outb[:, :, :]).then_inc(s["out_stored"], 16)
                sp.wait_ge(s["out_stored"], 16 * NCH)

            @block.gpsimd
            def _(pool):
                g = nc.gpsimd

                def chunk(c):
                    if not is_first(c):
                        wait_alone(pool, s["acc_done"], EX * TQ * c)
                    g.tensor_copy(wc[:, :, :], wts[:, bass.ds(c * TQ, TQ), :]).then_inc(s["chunk_ready"], 1)
                    g.tensor_copy(base[:, :, :], xs[:, bass.ds(c * TQ, TQ), :]).then_inc(s["chunk_ready"], 1)
                chunk(0)
                with pool.Fori(1, NCH) as c:
                    chunk(c)

            @block.scalar
            def _(act):
                a = nc.scalar

                def chunk(c):
                    for u in range(NU):
                        act.wait_ge(s["up_done"], NU * c + u + 1)
                        if not (is_first(c) and u < 2):
                            act.wait_ge(s["hid_done"], NU * c + u - 1)
                        a.activation(silu[u % 2][:, :], gb[UPB[u]][:, :], ACT.Silu).then_inc(s["silu_done"], 1)
                chunk(0)
                with act.Fori(1, NCH) as c:
                    chunk(c)

            @block.vector
            def _(dve):
                v = nc.vector

                def hidden(c, u):
                    e, k = divmod(u, KH)
                    dve.wait_ge(s["silu_done"], NU * c + u + 1)
                    if k == 0 and not (is_first(c) and e < 2):
                        dve.wait_ge(s["down_done"], EX * c + e - 1)
                    v.tensor_tensor(hid[e % 2][:, k, :], ub[UPB[u]][:, :], silu[u % 2][:, :], ALU.mult)\
                        .then_inc(s["hid_done"], 1)

                def combine(c, e):
                    dve.wait_ge(s["down_done"], EX * c + e + 1)
                    if e == 0:
                        dve.wait_ge(s["chunk_ready"], 2 * c + 2)
                    if e > 0:
                        dve.wait_ge(s["acc_done"], TQ * (EX * c + e))
                    if e == EX - 1 and not is_first(c):
                        dve.wait_ge(s["out_stored"], 16 * c)
                    src = base if e == 0 else acc
                    dst = outb if e == EX - 1 else acc
                    for t in range(TQ):
                        v.scalar_tensor_tensor(dst[:, t, :], ob[e % 2][:, t * P:(t + 1) * P], wc[:, t, e:e + 1],
                                               src[:, t, :], ALU.mult, ALU.add).then_inc(s["acc_done"], 1)

                def chunk(c):
                    for e in range(EX):
                        for k in range(KH):
                            hidden(c, e * KH + k)
                        if e > 0:
                            combine(c, e - 1)
                        elif not is_first(c):
                            combine(c - 1, EX - 1)
                chunk(0)
                with dve.Fori(1, NCH) as c:
                    chunk(c)
                combine(NCH - 1, EX - 1)

            @block.tensor
            def _(pe):
                t_ = nc.tensor

                def up(c, e):
                    for k in range(KH):
                        u = e * KH + k
                        if not (is_first(c) and u < 3):
                            pe.wait_ge(s["hid_done"], NU * c + since(UPB, u))
                        rhs = h2T[:, bass.ds(c * Q, Q)]
                        t_.matmul(gb[UPB[u]][:, :], w1_s[:, e, k * P:(k + 1) * P], rhs, start=True, stop=True)
                        t_.matmul(ub[UPB[u]][:, :], w2_s[:, e, k * P:(k + 1) * P], rhs, start=True, stop=True)\
                            .then_inc(s["up_done"], 1)

                def down(c, e):
                    pe.wait_ge(s["hid_done"], KH * (EX * c + e + 1))
                    if not (is_first(c) and e < 2):
                        pe.wait_ge(s["acc_done"], TQ * (EX * c + e - 1))
                    for t in range(TQ):
                        for k in range(KH):
                            last = t_.matmul(ob[e % 2][:, t * P:(t + 1) * P], hid[e % 2][:, k, t * P:(t + 1) * P],
                                             w3_s[:, e, k, :], start=k == 0, stop=k == KH - 1)
                    last.then_inc(s["down_done"], 1)

                def chunk(c):
                    for e in range(EX):
                        up(c, e)
                        if e > 0:
                            down(c, e - 1)
                        elif not is_first(c):
                            down(c - 1, EX - 1)
                chunk(0)
                with pe.Fori(1, NCH) as c:
                    chunk(c)
                down(NCH - 1, EX - 1)


_INS = ['x', 'Wq', 'bq', 'Wk', 'bk', 'Wv', 'bv', 'Wo', 'bo']
_FFN = ['ln1_scale', 'ln1_shift', 'wq', 'wk', 'wv', 'wo', 'bo', 'ln2_scale', 'ln2_shift', 'gate_w', 'w1', 'w2', 'w3']
_ALL = ['L0_attn_' + n for n in _INS] + ['L0_ffn_' + n for n in _FFN]


def kernel(**inputs):
    import numpy as _np
    import concourse.bacc as _bacc
    from concourse import mybir as _mybir
    from concourse.bass_utils import run_bass_kernel_spmd as _run

    nc = _bacc.Bacc("TRN2", target_bir_lowering=False, num_devices=1)
    arrays, args = {}, []
    for name in _ALL:
        a = _np.ascontiguousarray(inputs[name])
        arrays[f"in_{name}"] = a
        args.append(nc.dram_tensor(f"in_{name}", a.shape, _mybir.dt.from_np(a.dtype), kind="ExternalInput").ap())
    shape = inputs['L0_attn_x'].shape
    args.append(nc.dram_tensor("out_dram", shape, _mybir.dt.float32, kind="ExternalOutput").ap())
    preln_layer_kernel(nc, *args)
    r = _run(nc, [arrays], core_ids=[0])
    return r.results[0]["out_dram"]
```

```python
import concourse.bass as bass
from concourse import mybir
from contextlib import ExitStack


def preln_layer_kernel(nc: bass.Bass, x, Wq, bq, Wk, bk, Wv, bv, Wo, bo,
                       ln1_scale, ln1_shift, wq, wk, wv, wo, fbo,
                       ln2_scale, ln2_shift, gate_w, w1, w2, w3, out):
    fp32 = mybir.dt.float32
    bf16 = mybir.dt.bfloat16
    fp32r = mybir.dt.float32r
    ALU = mybir.AluOpType
    ACT = mybir.ActivationFunctionType
    X = mybir.AxisListType.X

    P = 128
    B, S, D = x.shape
    NT = B * S // P
    H, HD = 16, 8
    EX, HID = w1.shape[0], w1.shape[2]
    EPS = 1e-5
    HG = 4
    NG = B * H // HG
    TB = S // P
    Q = 512
    SCALE = HD ** -0.5
    MASKED = -3.0e38
    KS = 96
    KM = 98
    PARTS = [(0, 0), (0, 1), (0, 2), (1, 0), (1, 1), (2, 0)]
    CH = 2
    NC = NT // CH
    W = CH * P

    def wait_alone(eng, semaphore, count):
        eng.wait_ge(semaphore, count)
        if not isinstance(count, int):
            eng.sem_inc(passed)

    def skewed(eng, fs, order=None, peeled=0):
        order = order or list(reversed(range(len(fs))))
        lag = len(fs) - 1
        peeled = max(peeled, lag)

        def stages(i):
            for k in order:
                if fs[k] and not (isinstance(i, int) and not 0 <= i - k < NC):
                    fs[k](i - k)
        for i in range(peeled):
            stages(i)
        with eng.Fori(peeled, NC) as i:
            stages(i)
        for i in range(NC, NC + lag):
            stages(i)

    def first(i, n=1):
        return isinstance(i, int) and i < n

    MAXU = []
    for c in (1, 0):
        for t in range(4 * c, TB):
            w = min(Q, (t + 1) * P - c * Q)
            n = {128: 4, 256: 2}.get(w, 1)
            MAXU += [(t, c, i, n, w) for i in range(0, HG, n)]
    EXPG = []
    for c in (1, 0):
        for j in range(4 * (c + 1)):
            w = (c + 1) * Q - max(c * Q, j * P)
            EXPG.append((c, j, w, j >= 4 * c))
    EXPU = [(n, i, {128: 4, 256: 2}.get(EXPG[n][2], 1)) for n in range(len(EXPG))
            for i in range(0, HG, {128: 4, 256: 2}.get(EXPG[n][2], 1))]
    NMU, NEU, NEG = len(MAXU), len(EXPU), len(EXPG)
    LATE_UNITS = sum(1 for u in EXPU if EXPG[u[0]][0] == 1)
    LATE_KEYS = sum(1 for u in MAXU if u[1] == 1)
    NDG = sum(g[3] for g in EXPG)
    UNITS_UNTIL = [sum(1 for u in EXPU if u[0] <= n) for n in range(NEG)]
    DIAG_UNTIL = [sum(g[3] for g in EXPG[:n + 1]) for n in range(NEG)]

    def since(ring, u):
        before = [v for v in range(u) if ring[v] == ring[u]]
        if before:
            return before[-1] + 1
        return max(v for v in range(len(ring)) if ring[v] == ring[u]) + 1 - len(ring)


    PV_LAG = 2
    AHEAD = 5
    MAX_BY = 31
    AHEAD_FROM = 34

    def turn_order():
        order, m, e, turn_at = [], AHEAD, 0, NEG
        for n in range(NEG):
            if n == PV_LAG:
                order.append(("copy_ctx", 1))
            if n == 8 + PV_LAG:
                order.append(("copy_ctx", 0))
            for u in [u for u in EXPU if u[0] == n]:
                order.append(("exp", e))
                e += 1
                while m < min(NMU, AHEAD + -(-e * (NMU - AHEAD) // MAX_BY)):
                    order.append(("max", m))
                    m += 1
                if AHEAD_FROM <= e and m < NMU + AHEAD:
                    order.append(("max_ahead", m - NMU))
                    m += 1
            if m >= NMU and turn_at == NEG:
                order.append(("negate_max", 0))
                turn_at = n + 1
            order.append(("pv", n - PV_LAG))
            if n == turn_at:
                order.append(("turn_max", 0))
            if n == PV_LAG + 1:
                order.append(("turn_ctx", 1))
            if n == NEG - 1:
                order.append(("turn_ctx", 0))
        for u in range(max(m - NMU, 0), AHEAD):
            order.append(("max_ahead", u))
        return order
    TURN = turn_order()
    EXPB = [e % 3 for e in range(NEU)]
    MAXB = [m % 3 for m in range(NMU)]

    ctx = ExitStack()
    with ctx:
        def sb(name, shape, dt=fp32):
            return ctx.enter_context(nc.sbuf_tensor(name, shape, dt))

        def sem(name):
            return ctx.enter_context(nc.semaphore(name))

        banks = [ctx.enter_context(nc.psum_tensor(f"bank{i}", [P, Q], fp32)) for i in range(8)]
        NP = len(PARTS)
        qparts = nc.dram_tensor("qparts", (2, B, NP, H // HG, HD, HG * Q), bf16, kind="Internal").ap()
        kparts = nc.dram_tensor("kparts", (2, B, NP, H // HG, HD, HG * Q), bf16, kind="Internal").ap()

        xs = sb("xs", [P, NT, D])
        yb = sb("yb", [P, NT, D])
        vs = sb("vs", [P, NT, D])
        att = sb("att", [P, NT, D])
        bn = sb("bn", [P, NT, 6])
        stats1 = sb("stats1", [P, NT, 2])
        rstd1 = sb("rstd1", [P, NT])
        ident = sb("ident", [P, P])
        identb = sb("identb", [P, P], bf16)
        headones = sb("headones", [P, P])
        maskb = sb("maskb", [P, P], bf16)
        power = sb("power", [P, NT])
        Wq_s, Wk_s, Wv_s, Wo_s = (sb(n, [P, D]) for n in ("Wq_s", "Wk_s", "Wv_s", "Wo_s"))
        wq_s, wk_s, wv_s, wo_s = (sb(n, [P, D]) for n in ("wq_s", "wk_s", "wv_s", "wo_s"))
        cols = sb("cols", [P, 7])
        bq_c, bk_c, bv_c, s1_c, t1_c, s2_c, t2_c = (cols[:, i:i + 1] for i in range(7))
        bo_r = sb("bo_r", [P, D])
        fbo_r = sb("fbo_r", [P, D])

        w1_s = sb("w1_s", [P, EX, HID])
        w2_s = sb("w2_s", [P, EX, HID])
        w3_s = sb("w3_s", [P, EX, HID // P, D])
        gate_s = sb("gate_s", [P, EX])
        ffn_in = sem("ffn_weights_loaded")
        passed = sem("passed")
        w_in = sem("weights_loaded")
        consts = sem("consts_ready")

        operands = ctx.enter_context(ExitStack())
        NS = 2
        qop = [operands.enter_context(nc.sbuf_tensor(f"qop{i}", [P, 2, HG, Q], bf16)) for i in range(NS)]
        kop = [operands.enter_context(nc.sbuf_tensor(f"kop{i}", [P, 2, HG, Q], bf16)) for i in range(NS)]
        vop = [operands.enter_context(nc.sbuf_tensor(f"vop{i}", [P, TB, HG, 32], fp32)) for i in range(NS)]
        cleared = sem("operands_cleared")

        with ExitStack() as mix, nc.Block() as block:
            def mb(name, shape, dt=fp32):
                return mix.enter_context(nc.sbuf_tensor(name, shape, dt))

            RING = 4
            PAIR = Q // W
            st0 = mb("st0", [P, NT, 2])
            ve0 = mb("ve0", [P, NT])
            rs0 = mb("rs0", [P, NT])
            h0 = mb("h0", [P, CH, D])
            h0T = mb("h0T", [P, W])
            sqa = mb("sqa", [P, W])
            sqb = mb("sqb", [P, W])
            sqs = mb("sqs", [P, W])
            eqk = mb("eqk", [P, W])
            ov = mb("ov", [P, W])
            ve1 = mb("ve1", [P, NT])
            ve2 = mb("ve2", [P, NT])
            rr = mb("rr", [P, NT])
            hh = mb("hh", [P, CH, D])
            hT = mb("hT", [P, W])
            wq_p = mb("wq_p", [P, D])
            wk_p = mb("wk_p", [P, D])
            qp = mb("qp", [P, RING // PAIR, 3, PAIR * W], bf16)
            kp = mb("kp", [P, RING // PAIR, 3, PAIR * W], bf16)
            qr = mb("qr", [P, RING, W])
            kr = mb("kr", [P, RING, W])

            def part_of(parts, i, n):
                return parts[:, i // PAIR % 2, n, bass.ds(i % PAIR * W, W)]
            bT0, bAB, bV, bC, bO, bT1, bQK, bV2 = banks

            x_in = [sem(f"x_loaded{b}") for b in range(B)]
            names = ["bn0_done", "st0_done", "ve0_done", "rs0_done", "h0_done", "h0_turned", "h0T_done", "ab_done",
                     "vproj_done", "sq_done", "sqsum_done", "vb_done", "eqk_done", "coeff_done", "ov_done",
                     "wo_done", "xbo_done", "x1_done", "bn1_done", "st1_done", "ve1_done", "ve2_done", "rstd1_done",
                     "rr_done", "hh_done", "hh_turned", "hT_done", "qk_done", "v_done", "part1_done",
                     "rest_done", "part2_done", "part3_done", "vs_done", "qparts_stored", "kparts_stored", "order_done"]
            s = {n: sem(n) for n in names}

            @block.sync
            def _(sp):
                xv = x.rearrange("b (t p) d -> b p t d", p=P)
                for b in range(B):
                    sp.dma_start(xs[:, b * TB:(b + 1) * TB, :], xv[b]).then_inc(x_in[b], 16)
                for dst, src in ((Wq_s, Wq), (Wk_s, Wk), (Wv_s, Wv), (Wo_s, Wo),
                                 (wq_s, wq), (wk_s, wk), (wv_s, wv), (wo_s, wo)):
                    sp.dma_start(dst[:, :], src).then_inc(w_in, 16)
                for dst, src in ((bq_c, bq), (bk_c, bk), (bv_c, bv), (s1_c, ln1_scale), (t1_c, ln1_shift),
                                 (s2_c, ln2_scale), (t2_c, ln2_shift)):
                    sp.dma_start(dst, src.rearrange("(p a) -> p a", a=1)).then_inc(w_in, 16)
                for dst, src in ((bo_r, bo), (fbo_r, fbo)):
                    sp.dma_start(dst[:, :], src.partition_broadcast(P)).then_inc(w_in, 16)
                qd = qparts.rearrange("h b n g d (i t) -> h b (g d i) n t", i=HG)
                kd = kparts.rearrange("h b n g d (i t) -> h b (g d i) n t", i=HG)

                def store(j):
                    wait_alone(sp, s["part3_done"], 2 * PAIR * (j + 1))
                    if not first(j):
                        wait_alone(sp, s["qparts_stored"], 48 * j)
                        wait_alone(sp, s["kparts_stored"], 48 * j)
                    n = 0
                    for part, times in ((0, 3), (1, 2), (2, 1)):
                        sp.dma_start(qd[j % 2, j // 2, :, n:n + times, :],
                                     qp[:, j % 2, part].unsqueeze(1).to_broadcast([P, times, Q]))\
                            .then_inc(s["qparts_stored"], 16)
                        sp.dma_start(kd[j % 2, j // 2, :, n:n + times, :], kp[:, j % 2, 0:times])\
                            .then_inc(s["kparts_stored"], 16)
                        n += times
                store(0)
                with sp.Fori(1, NC // PAIR) as j:
                    store(j)
                sp.wait_ge(s["qparts_stored"], 48 * NC // PAIR)
                sp.wait_ge(s["kparts_stored"], 48 * NC // PAIR)

            @block.gpsimd
            def _(pool):
                g = nc.gpsimd
                g.memset(power[:, :], -0.5).then_inc(consts, 1)
                g.memset(ident[:, :], 0.0).then_inc(consts, 1)
                g.memset(headones[:, :], 1.0).then_inc(consts, 1)
                g.memset(maskb[:, :], 0.0).then_inc(consts, 1)
                pool.wait_ge(consts, 4)
                g.affine_select(out=ident[:, :], in_=ident[:, :], compare_op=ALU.not_equal, fill=1.0,
                                base=0, pattern=[[-1, P]], channel_multiplier=1).then_inc(consts, 1)
                hv = headones[:, :].rearrange("p (h d) -> p h d", d=HD)
                g.affine_select(out=hv, in_=hv, compare_op=ALU.is_ge, fill=0.0, base=0,
                                pattern=[[-HD, H], [0, HD]], channel_multiplier=1).then_inc(consts, 1)
                g.affine_select(out=maskb[:, :], in_=maskb[:, :], compare_op=ALU.is_ge, fill=MASKED,
                                base=0, pattern=[[-1, P]], channel_multiplier=1).then_inc(consts, 1)
                pool.wait_ge(consts, 7)
                g.affine_select(out=hv, in_=hv, compare_op=ALU.is_ge, fill=0.0, base=HD - 1,
                                pattern=[[HD, H], [0, HD]], channel_multiplier=-1).then_inc(consts, 1)
                g.tensor_copy(identb[:, :], ident[:, :]).then_inc(consts, 1)
                pool.wait_ge(s["ve0_done"], 1)
                g.tensor_tensor(rs0[:, :], ve0[:, :], power[:, :], ALU.pow).then_inc(s["rs0_done"], 1)
                for i in range(NS):
                    for a in (qop[i][:, :, :, :], vop[i][:, :, :, :]):
                        g.memset(a, 0.0).then_inc(cleared, 1)
                pool.wait_ge(cleared, 3 * NS)
                for i in range(NS):
                    g.memset(kop[i][KS:KM, :, :, :], 1.0).then_inc(cleared, 1)
                pool.wait_ge(cleared, 4 * NS)
                for i in range(NS):
                    g.memset(vop[i][:, :, :, HD:HD + 1], 1.0).then_inc(cleared, 1)
                pool.wait_ge(w_in, 16 * 17)

                def add_bias(i):
                    wait_alone(pool, s["h0_done"], CH * (i + 1))
                    xc = xs[:, bass.ds(CH * i, CH), :]
                    g.tensor_tensor(xc, xc, bo_r[:, :].unsqueeze(1).to_broadcast([P, CH, D]), ALU.add)\
                        .then_inc(s["xbo_done"], 1)
                skewed(pool, [None, add_bias, None, None, None, None, None])
                pool.wait_ge(s["ve2_done"], 1)
                g.tensor_tensor(rr[:, :], ve2[:, :], power[:, :], ALU.pow).then_inc(s["rr_done"], 1)
                pool.wait_ge(s["ve1_done"], 1)
                g.tensor_tensor(rstd1[:, :], ve1[:, :], power[:, :], ALU.pow).then_inc(s["rstd1_done"], 1)

                def part3(i):
                    for n, (parts, rest) in enumerate(((qp, qr), (kp, kr))):
                        wait_alone(pool, s["part2_done"], 2 * i + n + 1)
                        g.tensor_tensor(part_of(parts, i, 2), rest[:, i % RING, :], part_of(parts, i, 1),
                                        ALU.subtract).then_inc(s["part3_done"], 1)
                skewed(pool, [None, None, None, None, part3])

            @block.vector
            def _(dve):
                v = nc.vector
                for i in range(NS):
                    v.memset(kop[i][:, :, :, :], 0.0).then_inc(cleared, 1)
                for b in range(B):
                    dve.wait_ge(x_in[b], 16)
                    for t in range(b * TB, (b + 1) * TB):
                        v.bn_stats(bn[:, t, :], xs[:, t, :]).then_inc(s["bn0_done"], 1)
                dve.wait_ge(s["bn0_done"], NT)
                for t in range(NT):
                    v.bn_aggr(st0[:, t, :], bn[:, t, :]).then_inc(s["st0_done"], 1)
                dve.wait_ge(s["st0_done"], NT)
                v.tensor_scalar(ve0[:, :], st0[:, :, 1], EPS, None, ALU.add).then_inc(s["ve0_done"], 1)
                dve.wait_ge(s["rs0_done"], 1)

                def norm_x(i):
                    if not first(i):
                        dve.wait_ge(s["h0_turned"], i)
                    for t in range(CH):
                        v.tensor_scalar(h0[:, t, :], xs[:, CH * i + t, :], st0[:, CH * i + t, 0:1],
                                        rs0[:, bass.ds(CH * i + t, 1)], ALU.subtract, ALU.mult)\
                            .then_inc(s["h0_done"], 1)

                def square_sum(i):
                    dve.wait_ge(s["sq_done"], 2 * i + 2)
                    if not first(i):
                        dve.wait_ge(s["eqk_done"], i)
                    v.tensor_tensor(sqs[:, :], sqa[:, :], sqb[:, :], ALU.add).then_inc(s["sqsum_done"], 1)

                def mix(i):
                    dve.wait_ge(s["coeff_done"], i + 1)
                    dve.wait_ge(s["vb_done"], i + 1)
                    if not first(i):
                        dve.wait_ge(s["wo_done"], i)
                    vb = att[:, bass.ds(CH * i, CH), :].rearrange("p t d -> p (t d)")
                    v.tensor_tensor(ov[:, :], bC[:, 0:W], vb, ALU.mult).then_inc(s["ov_done"], 1)

                def make_x1(i):
                    dve.wait_ge(s["wo_done"], i + 1)
                    dve.wait_ge(s["xbo_done"], i + 1)
                    x1 = xs[:, bass.ds(CH * i, CH), :]
                    v.tensor_tensor(x1, bO[:, 0:W].rearrange("p (t d) -> p t d", t=CH), x1,
                                    ALU.add).then_inc(s["x1_done"], 1)

                def x1_stats(i):
                    wait_alone(dve, s["x1_done"], i + 1)
                    for t in range(CH):
                        v.bn_stats(bn[:, CH * i + t, :], xs[:, CH * i + t, :]).then_inc(s["bn1_done"], 1)
                skewed(dve, [norm_x, None, None, square_sum, mix, make_x1, x1_stats], [3, 5, 4, 0, 6])
                dve.wait_ge(s["bn1_done"], NT)
                for t in range(NT):
                    v.bn_aggr(stats1[:, t, :], bn[:, t, :]).then_inc(s["st1_done"], 1)
                dve.wait_ge(s["st1_done"], NT)
                var = stats1[:, :, 1]
                v.tensor_scalar(ve2[:, :], var, 1.0 + EPS, EPS * EPS, ALU.mult, ALU.add).then_inc(s["ve2_done"], 1)
                v.tensor_scalar(ve1[:, :], var, EPS, None, ALU.add).then_inc(s["ve1_done"], 1)
                dve.wait_ge(s["rr_done"], 1)

                def norm_x1(i):
                    if not first(i):
                        dve.wait_ge(s["hh_turned"], i)
                    for t in range(CH):
                        v.tensor_scalar(hh[:, t, :], xs[:, CH * i + t, :], stats1[:, CH * i + t, 0:1],
                                        rr[:, bass.ds(CH * i + t, 1)], ALU.subtract, ALU.mult)\
                            .then_inc(s["hh_done"], 1)

                def rests(i):
                    dve.wait_ge(s["part1_done"], 2 * i + 2)
                    for n, (parts, rest) in enumerate(((qp, qr), (kp, kr))):
                        if not first(i, RING):
                            dve.wait_ge(s["part3_done"], 2 * (i - RING) + n + 1)
                        v.tensor_tensor(rest[:, i % RING, :], bQK[:, n * W:(n + 1) * W], part_of(parts, i, 0),
                                        ALU.subtract).then_inc(s["rest_done"], 1)

                def part2(i):
                    for n, (parts, rest) in enumerate(((qp, qr), (kp, kr))):
                        dve.wait_ge(s["rest_done"], 2 * i + n + 1)
                        v.tensor_copy(part_of(parts, i, 1), rest[:, i % RING, :]).then_inc(s["part2_done"], 1)
                skewed(dve, [norm_x1, None, None, rests, part2], peeled=RING + 3)

            @block.scalar
            def _(act):
                a = nc.scalar
                act.wait_ge(w_in, 16 * 17)
                for dst, src in ((wq_p, wq_s), (wk_p, wk_s)):
                    a.copy(dst[:, :].rearrange("p (g d i) -> p g d i", d=HD, i=HG),
                           src[:, :].rearrange("p (g i d) -> p g d i", d=HD, i=HG)).then_inc(s["order_done"], 1)

                def turned(i):
                    act.wait_ge(s["h0_turned"], i + 1)
                    if not first(i):
                        act.wait_ge(s["vproj_done"], i)
                    a.copy(h0T[:, :], bT0[:, 0:W]).then_inc(s["h0T_done"], 1)

                def squares(i):
                    act.wait_ge(s["ab_done"], i + 1)
                    if not first(i):
                        act.wait_ge(s["sqsum_done"], i)
                    a.activation(sqa[:, :], bAB[:, 0:W], ACT.Square, bias=bq_c).then_inc(s["sq_done"], 1)
                    a.activation(sqb[:, :], bAB[:, W:2 * W], ACT.Square, bias=bk_c).then_inc(s["sq_done"], 1)
                    act.wait_ge(s["vproj_done"], i + 1)
                    vb = att[:, bass.ds(CH * i, CH), :].rearrange("p t d -> p (t d)")
                    a.activation(vb, bV[:, 0:W], ACT.Identity, bias=bv_c).then_inc(s["vb_done"], 1)

                def exponential(i):
                    act.wait_ge(s["sqsum_done"], i + 1)
                    if not first(i):
                        act.wait_ge(s["coeff_done"], i)
                    a.activation(eqk[:, :], sqs[:, :], ACT.Exp, scale=-0.5).then_inc(s["eqk_done"], 1)
                skewed(act, [None, turned, squares, exponential, None, None, None])

                def scale_shift(i):
                    act.wait_ge(s["hh_turned"], i + 1)
                    if not first(i):
                        act.wait_ge(s["v_done"], i)
                    a.activation(hT[:, :], bT1[:, 0:W], ACT.Identity, bias=t1_c, scale=s1_c).then_inc(s["hT_done"], 1)

                def part1(i):
                    act.wait_ge(s["qk_done"], i + 1)
                    for n, (parts, stored) in enumerate(((qp, s["qparts_stored"]), (kp, s["kparts_stored"]))):
                        if not first(i, RING):
                            act.wait_ge(stored, 48 * ((i - RING) // PAIR + 1))
                        a.copy(part_of(parts, i, 0), bQK[:, n * W:(n + 1) * W]).then_inc(s["part1_done"], 1)
                    act.wait_ge(s["v_done"], i + 1)
                    a.copy(vs[:, bass.ds(CH * i, CH), :], bV2[:, 0:W].rearrange("p (t d) -> p t d", t=CH))\
                        .then_inc(s["vs_done"], 1)
                skewed(act, [None, scale_shift, part1, None, None], peeled=RING + 2)

            @block.tensor
            def _(pe):
                t_ = nc.tensor
                pe.wait_ge(consts, 9)
                pe.wait_ge(w_in, 16 * 17)
                pe.wait_ge(s["order_done"], 2)

                def turn(i):
                    pe.wait_ge(s["h0_done"], CH * (i + 1))
                    if not first(i):
                        pe.wait_ge(s["h0T_done"], i)
                    for t in range(CH):
                        last = t_.transpose(bT0[:, t * P:(t + 1) * P], h0[:, t, :], ident[:, :])
                    last.then_inc(s["h0_turned"], 1)

                def project(i):
                    pe.wait_ge(s["h0T_done"], i + 1)
                    if not first(i):
                        pe.wait_ge(s["sq_done"], 2 * i)
                    t_.matmul(bAB[:, 0:W], Wq_s[:, :], h0T[:, :], start=True, stop=True)
                    t_.matmul(bAB[:, W:2 * W], Wk_s[:, :], h0T[:, :], start=True, stop=True).then_inc(s["ab_done"], 1)
                    if not first(i):
                        pe.wait_ge(s["vb_done"], i)
                    t_.matmul(bV[:, 0:W], Wv_s[:, :], h0T[:, :], start=True, stop=True).then_inc(s["vproj_done"], 1)

                def coeff(i):
                    pe.wait_ge(s["eqk_done"], i + 1)
                    if not first(i):
                        pe.wait_ge(s["ov_done"], i)
                    t_.matmul(bC[:, 0:W], headones[:, :], eqk[:, :], start=True, stop=True).then_inc(s["coeff_done"], 1)

                def mix_out(i):
                    pe.wait_ge(s["ov_done"], i + 1)
                    if not first(i):
                        pe.wait_ge(s["x1_done"], i)
                    for t in range(CH):
                        last = t_.matmul(bO[:, t * P:(t + 1) * P], ov[:, t * P:(t + 1) * P], Wo_s[:, :],
                                         start=True, stop=True)
                    last.then_inc(s["wo_done"], 1)
                skewed(pe, [None, turn, project, None, coeff, mix_out, None])

                def turn2(i):
                    pe.wait_ge(s["hh_done"], CH * (i + 1))
                    if not first(i):
                        pe.wait_ge(s["hT_done"], i)
                    for t in range(CH):
                        last = t_.transpose(bT1[:, t * P:(t + 1) * P], hh[:, t, :], ident[:, :])
                    last.then_inc(s["hh_turned"], 1)

                def heads(i):
                    pe.wait_ge(s["hT_done"], i + 1)
                    if not first(i):
                        pe.wait_ge(s["rest_done"], 2 * i)
                    t_.matmul(bQK[:, 0:W], wq_p[:, :], hT[:, :], start=True, stop=True)
                    t_.matmul(bQK[:, W:2 * W], wk_p[:, :], hT[:, :], start=True, stop=True).then_inc(s["qk_done"], 1)
                    if not first(i):
                        pe.wait_ge(s["vs_done"], i)
                    for t in range(CH):
                        last = t_.matmul(bV2[:, t * P:(t + 1) * P], hT[:, t * P:(t + 1) * P], wv_s[:, :],
                                         start=True, stop=True)
                    last.then_inc(s["v_done"], 1)
                skewed(pe, [None, turn2, heads, None, None], [1, 2])

        with ExitStack() as at, nc.Block() as block:
            def ab(name, shape, dt=fp32):
                return at.enter_context(nc.sbuf_tensor(name, shape, dt))

            NB = 4
            probs = [ab(f"probs{i}", [P, HG, Q]) for i in range(NB)]
            negmax = ab("negmax", [P, 2, HG, TB // 2])
            negmax1 = ab("negmax1", [P, HG, TB // 2])
            negparts = ab("negparts", [P, 2, 2, HG, TB // 2], bf16)
            negrows = ab("negrows", [2 * HG * TB, P], bf16)
            ctxT = ab("ctxT", [P, Q])
            recip = ab("recip", [P, 4, HG])
            centred = ab("centred", [P, CH, D])
            scaled = ab("scaled", [P, CH, D])
            expb, maxb, pvb, miscb = banks[0:3], banks[3:6], banks[6], banks[7]

            late_in = [sem(f"late_operands_loaded{i}") for i in range(NS)]
            early_in = [sem(f"early_operands_loaded{i}") for i in range(NS)]
            rows_in = [sem(f"maxrows_loaded{i}") for i in range(NS)]
            names = ["st_done", "exp_done", "select_done", "vop_ready", "pv_done",
                     "ctx_out", "ctx_turned", "recip_done", "ctx_done", "max_done", "maxred_done", "negmax_done",
                     "neghi_done", "neglo_done", "neg_turned", "neg_out", "residual_step"]
            s = {n: sem(n) for n in names}

            def turns(eng, body):
                body(0, 0, 0)
                with eng.Fori(0, NG // 2 - 2) as p:
                    body(2 * p + 1, p, 1)
                    body(2 * p + 2, p + 1, 0)
                for g in range(NG - 3, NG):
                    body(g, g // 2, g % 2)

            def is_first(g):
                return isinstance(g, int) and g == 0

            def is_last(g):
                return isinstance(g, int) and g == NG - 1

            def has_two_after(g):
                return not (isinstance(g, int) and g + 2 >= NG)

            def nxt(g, k, par):
                return g + 1, (k if par < NS - 1 else k + 1), (par + 1) % NS

            @block.sync
            def _(sp):
                def load(g, par, half):
                    for op, parts in ((kop, kparts), (qop, qparts)):
                        sp.dma_start(op[par][0:NP * HD, half].rearrange("p i t -> p (i t)"),
                                     parts[half, g // 4, :, g % 4]).then_inc((late_in if half else early_in)[par], 16)

                def max_rows(g, k, par):
                    sp.wait_ge(s["neg_out"], g + 1)
                    sp.dma_start(qop[par][KS:KM].rearrange("p h i q -> p (h i q)"), negrows[:, :])\
                        .then_inc(rows_in[par], 16)
                for g in range(NS):
                    load(g, g, 1)
                    load(g, g, 0)
                max_rows(0, 0, 0)

                sp.dma_start(gate_s[:, :], gate_w).then_inc(ffn_in, 16)
                sp.dma_start(w1_s[:, :, :], w1.rearrange("e d h -> d e h")).then_inc(ffn_in, 16)
                sp.dma_start(w2_s[:, :, :], w2.rearrange("e d h -> d e h")).then_inc(ffn_in, 16)
                for k in range(HID // P):
                    sp.dma_start(w3_s[:, :, k, :], w3[:, k * P:(k + 1) * P, :].rearrange("e h d -> h e d"))\
                        .then_inc(ffn_in, 16)

                def turn(g, k, par):
                    more = has_two_after(g)
                    if more:
                        wait_alone(sp, s["st_done"], NEU * g + LATE_UNITS)
                        load(g + 2, par, 1)
                    if not is_last(g):
                        max_rows(*nxt(g, k, par))
                    if more:
                        wait_alone(sp, s["st_done"], NEU * (g + 1))
                        load(g + 2, par, 0)
                turns(sp, turn)

            @block.gpsimd
            def _(pool):
                g_ = nc.gpsimd
                def vcopy(g, k, par):
                    if not (isinstance(g, int) and g < 2):
                        wait_alone(pool, s["pv_done"], NEG * (g - 1))
                    src = vs[:, bass.ds((g // 4) * TB, TB), bass.ds((g % 4) * HG * HD, HG * HD)]
                    g_.tensor_copy(vop[par][:, :, :, 0:HD], src.rearrange("p t (i d) -> p t i d", d=HD))\
                        .then_inc(s["vop_ready"], 1)
                vcopy(0, 0, 0)

                def residual(g, step):
                    xc, yc = (a[:, bass.ds(CH * g, CH), :] for a in (xs, yb))
                    mean = stats1[:, bass.ds(CH * g, CH), 0:1].to_broadcast([P, CH, D])
                    rstd = rstd1[:, bass.ds(CH * g, CH)].unsqueeze(2).to_broadcast([P, CH, D])
                    bias = fbo_r[:, :].unsqueeze(1).to_broadcast([P, CH, D])
                    out, a, b, op = ((centred[:, :, :], xc, mean, ALU.subtract),
                                     (scaled[:, :, :], centred[:, :, :], rstd, ALU.mult),
                                     (yc, scaled[:, :, :], bias, ALU.add),
                                     (xc, xc, yc, ALU.add))[step]
                    if not (is_first(g) and step == 0):
                        wait_alone(pool, s["residual_step"], 4 * g + step)
                    g_.tensor_tensor(out, a, b, op).then_inc(s["residual_step"], 1)

                def turn(g, k, par):
                    for n in range(NEG):
                        if n < 4:
                            residual(g, n)
                        if EXPG[n][3]:
                            wait_alone(pool, s["exp_done"], NEU * g + UNITS_UNTIL[n])
                            d = probs[n % NB][:, :, 0:P]
                            g_.affine_select(out=d, in_=d, compare_op=ALU.is_ge, fill=0.0, base=0,
                                             pattern=[[0, HG], [1, P]], channel_multiplier=-1)\
                                .then_inc(s["select_done"], 1)
                        if n == 6 and not is_last(g):
                            vcopy(*nxt(g, k, par))
                turns(pool, turn)

            @block.vector
            def _(dve):
                v = nc.vector
                def max_unit(g, m):
                    t, c, i, n, w = MAXU[m]
                    dve.wait_ge(s["max_done"], NMU * g + m + 1)
                    dst = negmax[:, t // 4, i:i + n, t % 4:t % 4 + 1] if c == 0 else negmax1[:, i:i + n, t - 4:t - 3]
                    src = maxb[MAXB[m]][:, 0:n * w].rearrange("p (i k) -> p i k", i=n)
                    v.tensor_reduce(dst, src, X, ALU.max, negate=True).then_inc(s["maxred_done"], 1)

                def row_max(g):
                    dve.wait_ge(s["maxred_done"], NMU * (g + 1))
                    late = negmax[:, 1, :, :]
                    v.tensor_tensor(late, late, negmax1[:, :, :], ALU.min).then_inc(s["negmax_done"], 1)
                    dve.wait_ge(s["negmax_done"], g + 1)
                    if not is_first(g):
                        dve.wait_ge(s["neg_turned"], g)
                    v.tensor_copy(negparts[:, 0], negmax[:, :, :, :]).then_inc(s["neghi_done"], 1)
                    dve.wait_ge(s["neghi_done"], g + 1)
                    v.tensor_tensor(negparts[:, 1], negmax[:, :, :, :], negparts[:, 0], ALU.subtract)\
                        .then_inc(s["neglo_done"], 1)

                def max_rows_out(g):
                    dve.wait_ge(s["neg_turned"], g + 1)
                    if not is_first(g):
                        dve.wait_ge(*rows_before(g))
                    v.tensor_copy(negrows[:, :], miscb[0:2 * HG * TB, 0:P // 2].bitcast(bf16))\
                        .then_inc(s["neg_out"], 1)

                par_of = {}

                def rows_before(g):
                    par, k = par_of["now"]
                    return rows_in[(par - 1) % NS], 16 * (k if par == 0 else k + 1)

                def normalize(g, half):
                    dve.wait_ge(s["ctx_turned"], 2 * g + half + 1)
                    cv = miscb[:, :].rearrange("p (t i c) -> p t i c", t=4, i=HG)
                    v.reciprocal(recip[:, :, :], cv[:, :, :, HD]).then_inc(s["recip_done"], 1)
                    dve.wait_ge(s["recip_done"], 2 * g + half + 1)
                    first_tile = (g // 4) * TB + (4 if half == 0 else 0)
                    dst = att[:, bass.ds(first_tile, 4), bass.ds((g % 4) * HG * HD, HG * HD)]
                    v.tensor_tensor(dst.rearrange("p t (i d) -> p t i d", d=HD), cv[:, :, :, 0:HD],
                                    recip[:, :, :].unsqueeze(3).to_broadcast([P, 4, HG, HD]), ALU.mult)\
                        .then_inc(s["ctx_done"], 1)

                par_of["now"] = (0, 0)
                for m in range(NMU):
                    max_unit(0, m)
                row_max(0)
                max_rows_out(0)
                for m in range(AHEAD):
                    max_unit(1, m)

                def turn(g, k, par):
                    for what, m in TURN:
                        if what == "max" and not is_last(g):
                            max_unit(g + 1, m)
                        if what == "max_ahead" and has_two_after(g):
                            max_unit(g + 2, m)
                        if what == "negate_max" and not is_last(g):
                            row_max(g + 1)
                        if what == "turn_max" and not is_last(g):
                            g1, k1, par1 = nxt(g, k, par)
                            par_of["now"] = (par1, k1)
                            max_rows_out(g1)
                        if what == "turn_ctx" and m == 1 and not is_first(g):
                            normalize(g - 1, 1)
                        if what == "turn_ctx" and m == 0:
                            normalize(g, 0)
                turns(dve, turn)
                normalize(NG - 1, 1)

            @block.scalar
            def _(act):
                a = nc.scalar

                def exp_unit(g, e):
                    n, i, heads = EXPU[e]
                    w = EXPG[n][2]
                    if i == 0 and not (is_first(g) and n < NB):
                        act.wait_ge(s["pv_done"], NEG * g + n - NB + 1)
                    act.wait_ge(s["st_done"], NEU * g + e + 1)
                    a.activation(probs[n % NB][:, i:i + heads, 0:w],
                                 expb[EXPB[e]][:, 0:heads * w].rearrange("p (i q) -> p i q", i=heads),
                                 ACT.Exp, scale=SCALE).then_inc(s["exp_done"], 1)

                def ctx_copy(g, half):
                    act.wait_ge(s["pv_done"], NEG * g + (8 if half == 0 else 12))
                    if not (is_first(g) and half == 0):
                        act.wait_ge(s["ctx_turned"], 2 * g + half)
                    a.copy(ctxT[:, :], pvb[:, :]).then_inc(s["ctx_out"], 1)

                def turn(g, k, par):
                    for what, m in TURN:
                        if what == "exp":
                            exp_unit(g, m)
                        if what == "copy_ctx" and m == 1 and not is_first(g):
                            ctx_copy(g - 1, 1)
                        if what == "copy_ctx" and m == 0:
                            ctx_copy(g, 0)
                turns(act, turn)
                ctx_copy(NG - 1, 1)

            @block.tensor
            def _(pe):
                t_ = nc.tensor

                def max_unit(g, k, par, m):
                    t, c, i, n, w = MAXU[m]
                    if m == 0:
                        pe.wait_ge(late_in[par], LOADS * (k + 1))
                    if m == LATE_KEYS:
                        pe.wait_ge(early_in[par], LOADS * (k + 1))
                    if not (is_first(g) and m < 3):
                        pe.wait_ge(s["maxred_done"], NMU * g + since(MAXB, m))
                    diag = c == 1 or t < 4
                    for h in range(n):
                        o = maxb[MAXB[m]][:, h * w:(h + 1) * w]
                        last = t_.matmul(o, qop[par][0:KS, t // 4, i + h, t % 4 * P:(t % 4 + 1) * P],
                                         kop[par][0:KS, c, i + h, 0:w], start=True, stop=not diag)
                        if diag:
                            last = t_.matmul(o[:, w - P:w], identb[:, :], maskb[:, :], start=False, stop=True)
                    last.then_inc(s["max_done"], 1)

                def st_unit(g, par, e):
                    n, i, heads = EXPU[e]
                    c, j, w, _ = EXPG[n]
                    if not (is_first(g) and e < 3):
                        pe.wait_ge(s["exp_done"], NEU * g + since(EXPB, e))
                    for h in range(heads):
                        last = t_.matmul(expb[EXPB[e]][:, h * w:(h + 1) * w], 
                                         kop[par][0:KM, j // 4, i + h, j % 4 * P:(j % 4 + 1) * P],
                                         qop[par][0:KM, c, i + h, Q - w:Q], start=True, stop=True)
                    last.then_inc(s["st_done"], 1)

                def pv_group(g, par, n):
                    c, j, w, diag = EXPG[n]
                    if n == 0:
                        pe.wait_ge(s["vop_ready"], g + 1)
                        if not is_first(g):
                            pe.wait_ge(s["ctx_out"], 2 * g)
                    if n == 8:
                        pe.wait_ge(s["ctx_out"], 2 * g + 1)
                    pe.wait_ge(s["exp_done"], NEU * g + UNITS_UNTIL[n])
                    if diag:
                        pe.wait_ge(s["select_done"], NDG * g + DIAG_UNTIL[n])
                    for i in range(HG):
                        last = t_.matmul(pvb[32 * i:32 * i + 32, Q - w:Q], vop[par][:, j, i, :],
                                         probs[n % NB][:, i, 0:w], start=j == 0, stop=j == 4 * c + 3)
                    last.then_inc(s["pv_done"], 1)

                def turn_ctx(g, half):
                    pe.wait_ge(s["ctx_out"], 2 * g + half + 1)
                    if half == 1:
                        pe.wait_ge(s["ctx_done"], 2 * g + 1)
                    elif is_last(g):
                        pe.wait_ge(s["ctx_done"], 2 * g)
                    else:
                        pe.wait_ge(s["neg_out"], g + 2)
                    for t in range(4):
                        last = t_.transpose(miscb[:, t * P:(t + 1) * P], ctxT[:, t * P:(t + 1) * P], ident[:, :])
                    last.then_inc(s["ctx_turned"], 1)

                def turn_max(g):
                    wait_alone(pe, s["neglo_done"], g + 1)
                    if isinstance(g, int) and g == 1:
                        pe.wait_ge(s["neg_out"], 1)
                    elif not is_first(g):
                        wait_alone(pe, s["ctx_done"], 2 * g - 2)
                    t_.transpose(miscb[0:2 * HG * TB, 0:P // 2].bitcast(bf16),
                                 negparts[:, :, :, :, :].rearrange("p a h i t -> p (a h i t)"), identb[:, :])\
                        .then_inc(s["neg_turned"], 1)

                LOADS = 2 * 16
                for m in range(NMU):
                    max_unit(0, 0, 0, m)
                turn_max(0)
                for m in range(AHEAD):
                    max_unit(1, 0, 1, m)

                def turn(g, k, par):
                    g1, k1, par1 = nxt(g, k, par)
                    pe.wait_ge(rows_in[par], 16 * (k + 1))
                    for what, m in TURN:
                        if what == "exp":
                            st_unit(g, par, m)
                        if what == "max" and not is_last(g):
                            max_unit(g1, k1, par1, m)
                        if what == "max_ahead" and has_two_after(g):
                            max_unit(*nxt(g1, k1, par1), m)
                        if what == "pv" and m >= 0:
                            pv_group(g, par, m)
                        if what == "pv" and m < 0 and not is_first(g):
                            pv_group(g - 1, (par - 1) % NS, NEG + m)
                        if what == "turn_ctx" and m == 1 and not is_first(g):
                            turn_ctx(g - 1, 1)
                        if what == "turn_ctx" and m == 0:
                            turn_ctx(g, 0)
                        if what == "turn_max" and not is_last(g):
                            turn_max(g1)
                turns(pe, turn)
                for n in range(NEG - PV_LAG, NEG):
                    pv_group(NG - 1, (NG - 1) % NS, n)
                turn_ctx(NG - 1, 1)

        operands.close()

        h2_head = sb("h2_head", [P, NT * P])
        h2_rest = sb("h2_rest", [P, NT * P])
        logits = sb("logits", [P, NT, EX])
        w1_head = sb("w1_head", [P, EX, HID])
        w2_head = sb("w2_head", [P, EX, HID])
        w1_rest = sb("w1_rest", [P, EX, HID])
        w2_rest = sb("w2_rest", [P, EX, HID])
        wts = sb("wts", [P, NT, EX])
        with ExitStack() as fi, nc.Block() as block:
            def fb(name, shape, dt=fp32):
                return fi.enter_context(nc.sbuf_tensor(name, shape, dt))

            attc = fb("attc", [P, CH, D])
            attT = fb("attT", [P, W])
            hzT = fb("hzT", [P, W])
            stats2 = fb("stats2", [P, NT, 2])
            vez = fb("vez", [P, NT])
            rstd2 = fb("rstd2", [P, NT])
            hz = fb("hz", [P, CH, D])
            rank = fb("rank", [P, EX])
            sel = fb("sel", [P, NT, EX])
            oh1 = fb("oh1", [P, NT, EX])
            oh2 = fb("oh2", [P, NT, EX])
            rest = fb("rest", [P, NT, EX])
            best = fb("best", [P, 2, NT])
            pick = fb("pick", [P, NT])
            gap = fb("gap", [P, NT])
            egap = fb("egap", [P, NT])
            eone = fb("eone", [P, NT])
            pr = fb("pr", [P, 2, NT])
            bA, bZ, bH, bG = banks[0:4]
            names = ["attc_done", "att_turned", "attT_done", "wo2_done", "z_done", "resid_done", "bn2_done",
                     "st2_done", "vez_done", "rstd2_done", "hz_done", "hz_turned", "hzT_done", "head_done", "h2T_done", "gate_done", "w_head_done", "w_rest_done",
                     "logits_done", "rank_done", "gap_done", "egap_done", "gating_step"]
            s = {n: sem(n) for n in names}

            @block.gpsimd
            def _(pool):
                g = nc.gpsimd
                for e in range(EX):
                    last = g.memset(rank[:, e:e + 1], float(EX - e))
                last.then_inc(s["rank_done"], 1)

                pool.wait_ge(s["vez_done"], 1)
                g.tensor_tensor(rstd2[:, :], vez[:, :], power[:, :], ALU.pow).then_inc(s["rstd2_done"], 1)

            @block.vector
            def _(dve):
                v = nc.vector

                def make_z(i):
                    zc, xc = (a[:, bass.ds(CH * i, CH), :] for a in (yb, xs))
                    o = bZ[:, 0:W].rearrange("p (t d) -> p t d", t=CH)
                    dve.wait_ge(s["wo2_done"], i + 1)
                    v.tensor_tensor(zc, o, zc, ALU.add).then_inc(s["z_done"], 1)
                    v.tensor_tensor(xc, o, xc, ALU.add).then_inc(s["resid_done"], 1)

                def z_stats(i):
                    wait_alone(dve, s["z_done"], i + 1)
                    for t in range(CH):
                        v.bn_stats(bn[:, CH * i + t, :], yb[:, CH * i + t, :]).then_inc(s["bn2_done"], 1)
                for n, (w, head, rest_) in enumerate(((w1_s, w1_head, w1_rest), (w2_s, w2_head, w2_rest))):
                    dve.wait_ge(s["w_head_done"], n + 1)
                    v.tensor_tensor(rest_[:, :, :].bitcast(fp32r), w[:, :, :], head[:, :, :], ALU.subtract)\
                        .then_inc(s["w_rest_done"], 1)
                skewed(dve, [None, None, make_z, z_stats])
                dve.wait_ge(s["bn2_done"], NT)
                for t in range(NT):
                    v.bn_aggr(stats2[:, t, :], bn[:, t, :]).then_inc(s["st2_done"], 1)
                dve.wait_ge(s["st2_done"], NT)
                v.tensor_scalar(vez[:, :], stats2[:, :, 1], EPS, None, ALU.add).then_inc(s["vez_done"], 1)
                dve.wait_ge(s["rstd2_done"], 1)

                def norm_z(i):
                    if not first(i):
                        dve.wait_ge(s["hz_turned"], i)
                    for t in range(CH):
                        v.tensor_scalar(hz[:, t, :], yb[:, CH * i + t, :], stats2[:, CH * i + t, 0:1],
                                        rstd2[:, bass.ds(CH * i + t, 1)], ALU.subtract, ALU.mult)\
                            .then_inc(s["hz_done"], 1)

                def keep(i):
                    dve.wait_ge(s["hzT_done"], i + 1)
                    head, rest = (a[:, bass.ds(i * W, W)] for a in (h2_head, h2_rest))
                    v.tensor_copy(head.bitcast(fp32r), hzT[:, :]).then_inc(s["head_done"], 1)
                    dve.wait_ge(s["head_done"], i + 1)
                    v.tensor_tensor(rest.bitcast(fp32r), hzT[:, :], head, ALU.subtract).then_inc(s["h2T_done"], 1)
                    dve.wait_ge(s["gate_done"], i + 1)
                    v.tensor_copy(logits[:, bass.ds(CH * i, CH), :],
                                  bG[:, 0:CH * EX].rearrange("p (t e) -> p t e", e=EX)).then_inc(s["logits_done"], 1)
                skewed(dve, [norm_z, None, keep])

                steps = [0]

                def step(ins):
                    steps[0] += 1
                    ins.then_inc(s["gating_step"], 1)
                    dve.wait_ge(s["gating_step"], steps[0])
                rk = rank[:, :].unsqueeze(1).to_broadcast([P, NT, EX])

                def wide(a):
                    return a.unsqueeze(2).to_broadcast([P, NT, EX])

                def choose(scores, m, onehot):
                    step(v.tensor_reduce(best[:, m, :], scores, X, ALU.max))
                    step(v.tensor_tensor(sel[:, :, :], scores, wide(best[:, m, :]), ALU.is_equal))
                    step(v.tensor_tensor(sel[:, :, :], sel[:, :, :], rk, ALU.mult))
                    step(v.tensor_reduce(pick[:, :], sel[:, :, :], X, ALU.max))
                    step(v.tensor_tensor(onehot[:, :, :], rk, wide(pick[:, :]), ALU.is_equal))
                dve.wait_ge(s["logits_done"], NC)
                dve.wait_ge(s["rank_done"], 1)
                choose(logits[:, :, :], 0, oh1)
                step(v.tensor_scalar(sel[:, :, :], oh1[:, :, :], -1.0, 1.0, ALU.mult, ALU.add))
                step(v.tensor_tensor(rest[:, :, :], logits[:, :, :], sel[:, :, :], ALU.mult))
                step(v.tensor_scalar(sel[:, :, :], oh1[:, :, :], MASKED, None, ALU.mult))
                step(v.tensor_tensor(rest[:, :, :], rest[:, :, :], sel[:, :, :], ALU.add))
                choose(rest[:, :, :], 1, oh2)
                v.tensor_tensor(gap[:, :], best[:, 1, :], best[:, 0, :], ALU.subtract).then_inc(s["gap_done"], 1)
                dve.wait_ge(s["egap_done"], 1)
                step(v.tensor_scalar(eone[:, :], egap[:, :], 1.0, None, ALU.add))
                step(v.reciprocal(pr[:, 0, :], eone[:, :]))
                step(v.tensor_tensor(pr[:, 1, :], pr[:, 0, :], egap[:, :], ALU.mult))
                step(v.tensor_tensor(oh1[:, :, :], oh1[:, :, :], wide(pr[:, 0, :]), ALU.mult))
                step(v.tensor_tensor(oh2[:, :, :], oh2[:, :, :], wide(pr[:, 1, :]), ALU.mult))
                step(v.tensor_tensor(wts[:, :, :], oh1[:, :, :], oh2[:, :, :], ALU.add))

            @block.scalar
            def _(act):
                a = nc.scalar

                def att_fetch(i):
                    if not first(i):
                        act.wait_ge(s["att_turned"], i)
                    a.copy(attc[:, :, :], att[:, bass.ds(CH * i, CH), :]).then_inc(s["attc_done"], 1)

                def att_copy(i):
                    act.wait_ge(s["att_turned"], i + 1)
                    if not first(i):
                        act.wait_ge(s["wo2_done"], i)
                    a.copy(attT[:, :], bA[:, 0:W]).then_inc(s["attT_done"], 1)
                act.wait_ge(ffn_in, 16 * 5)
                for w, head in ((w1_s, w1_head), (w2_s, w2_head)):
                    a.copy(head[:, :, :].bitcast(fp32r), w[:, :, :]).then_inc(s["w_head_done"], 1)
                skewed(act, [att_fetch, att_copy, None, None])

                def scale_shift(i):
                    act.wait_ge(s["hz_turned"], i + 1)
                    if not first(i):
                        act.wait_ge(s["gate_done"], i)
                        act.wait_ge(s["h2T_done"], i)
                    a.activation(hzT[:, :], bH[:, 0:W], ACT.Identity, bias=t2_c, scale=s2_c).then_inc(s["hzT_done"], 1)
                skewed(act, [None, scale_shift, None])
                act.wait_ge(s["gap_done"], 1)
                a.activation(egap[:, :], gap[:, :], ACT.Exp).then_inc(s["egap_done"], 1)

            @block.tensor
            def _(pe):
                t_ = nc.tensor

                def att_turn(i):
                    pe.wait_ge(s["attc_done"], i + 1)
                    if not first(i):
                        pe.wait_ge(s["attT_done"], i)
                    for t in range(CH):
                        last = t_.transpose(bA[:, t * P:(t + 1) * P], attc[:, t, :], ident[:, :])
                    last.then_inc(s["att_turned"], 1)

                def att_out(i):
                    pe.wait_ge(s["attT_done"], i + 1)
                    if not first(i):
                        pe.wait_ge(s["z_done"], i)
                        pe.wait_ge(s["resid_done"], i)
                    for t in range(CH):
                        last = t_.matmul(bZ[:, t * P:(t + 1) * P], attT[:, t * P:(t + 1) * P], wo_s[:, :],
                                         start=True, stop=True)
                    last.then_inc(s["wo2_done"], 1)
                skewed(pe, [None, att_turn, att_out, None])
                pe.wait_ge(ffn_in, 16 * 5)

                def z_turn(i):
                    pe.wait_ge(s["hz_done"], CH * (i + 1))
                    if not first(i):
                        pe.wait_ge(s["hzT_done"], i)
                    for t in range(CH):
                        last = t_.transpose(bH[:, t * P:(t + 1) * P], hz[:, t, :], ident[:, :])
                    last.then_inc(s["hz_turned"], 1)

                def gate(i):
                    pe.wait_ge(s["hzT_done"], i + 1)
                    if not first(i):
                        pe.wait_ge(s["logits_done"], i)
                    for t in range(CH):
                        last = t_.matmul(bG[:, t * EX:(t + 1) * EX], hzT[:, t * P:(t + 1) * P], gate_s[:, :],
                                         start=True, stop=True)
                    last.then_inc(s["gate_done"], 1)
                skewed(pe, [None, z_turn, gate])

        with ExitStack() as ff, nc.Block() as block:
            def eb(name, shape, dt=fp32):
                return ff.enter_context(nc.sbuf_tensor(name, shape, dt))

            NCH = NT * P // Q
            TQ = Q // P
            KH = HID // P
            NU = EX * KH
            silu = [eb(f"silu{i}", [P, Q]) for i in range(2)]
            hid = [eb(f"hid{i}", [P, KH, Q]) for i in range(2)]
            wc = eb("wc", [P, TQ, EX])
            base = eb("base", [P, TQ, D])
            acc = eb("acc", [P, TQ, D])
            outb = eb("outb", [P, TQ, D])
            gb, ub, ob = banks[0:3], banks[3:6], banks[6:8]
            UPB = [u % 3 for u in range(NU - 1)] + [1]
            names = ["up_done", "silu_done", "hid_done", "down_done", "acc_done", "chunk_ready", "out_stored"]
            s = {n: sem(n) for n in names}

            def is_first(c):
                return isinstance(c, int) and c == 0

            @block.sync
            def _(sp):
                ov = out.rearrange("b s d -> (b s) d").rearrange("(c t p) d -> c p t d", p=P, t=TQ)
                with sp.Fori(0, NCH) as c:
                    sp.wait_ge(s["acc_done"], EX * TQ * (c + 1))
                    sp.dma_start(ov[c], outb[:, :, :]).then_inc(s["out_stored"], 16)
                sp.wait_ge(s["out_stored"], 16 * NCH)

            @block.gpsimd
            def _(pool):
                g = nc.gpsimd

                def chunk(c):
                    if not is_first(c):
                        wait_alone(pool, s["acc_done"], EX * TQ * c)
                    g.tensor_copy(wc[:, :, :], wts[:, bass.ds(c * TQ, TQ), :]).then_inc(s["chunk_ready"], 1)
                    g.tensor_copy(base[:, :, :], xs[:, bass.ds(c * TQ, TQ), :]).then_inc(s["chunk_ready"], 1)
                chunk(0)
                with pool.Fori(1, NCH) as c:
                    chunk(c)

            @block.scalar
            def _(act):
                a = nc.scalar

                def chunk(c):
                    for u in range(NU):
                        act.wait_ge(s["up_done"], NU * c + u + 1)
                        if not (is_first(c) and u < 2):
                            act.wait_ge(s["hid_done"], NU * c + u - 1)
                        a.activation(silu[u % 2][:, :], gb[UPB[u]][:, :], ACT.Silu).then_inc(s["silu_done"], 1)
                chunk(0)
                with act.Fori(1, NCH) as c:
                    chunk(c)

            @block.vector
            def _(dve):
                v = nc.vector

                def hidden(c, u):
                    e, k = divmod(u, KH)
                    dve.wait_ge(s["silu_done"], NU * c + u + 1)
                    if k == 0 and not (is_first(c) and e < 2):
                        dve.wait_ge(s["down_done"], EX * c + e - 1)
                    v.tensor_tensor(hid[e % 2][:, k, :], ub[UPB[u]][:, :], silu[u % 2][:, :], ALU.mult)\
                        .then_inc(s["hid_done"], 1)

                def combine(c, e):
                    dve.wait_ge(s["down_done"], EX * c + e + 1)
                    if e == 0:
                        dve.wait_ge(s["chunk_ready"], 2 * c + 2)
                    if e > 0:
                        dve.wait_ge(s["acc_done"], TQ * (EX * c + e))
                    if e == EX - 1 and not is_first(c):
                        dve.wait_ge(s["out_stored"], 16 * c)
                    src = base if e == 0 else acc
                    dst = outb if e == EX - 1 else acc
                    for t in range(TQ):
                        v.scalar_tensor_tensor(dst[:, t, :], ob[e % 2][:, t * P:(t + 1) * P], wc[:, t, e:e + 1],
                                               src[:, t, :], ALU.mult, ALU.add).then_inc(s["acc_done"], 1)

                def chunk(c):
                    for e in range(EX):
                        for k in range(KH):
                            hidden(c, e * KH + k)
                        if e > 0:
                            combine(c, e - 1)
                        elif not is_first(c):
                            combine(c - 1, EX - 1)
                chunk(0)
                with dve.Fori(1, NCH) as c:
                    chunk(c)
                combine(NCH - 1, EX - 1)

            @block.tensor
            def _(pe):
                t_ = nc.tensor

                def up(c, e):
                    for k in range(KH):
                        u = e * KH + k
                        if not (is_first(c) and u < 3):
                            pe.wait_ge(s["hid_done"], NU * c + since(UPB, u))
                        for o, w_head, w_rest in ((gb, w1_head, w1_rest), (ub, w2_head, w2_rest)):
                            products = ((w_head, h2_head), (w_head, h2_rest), (w_rest, h2_head))
                            for n, (w, h) in enumerate(products):
                                last = t_.matmul(o[UPB[u]][:, :], w[:, e, k * P:(k + 1) * P].bitcast(fp32r),
                                                 h[:, bass.ds(c * Q, Q)].bitcast(fp32r), start=n == 0, stop=n == 2)
                        last.then_inc(s["up_done"], 1)

                def down(c, e):
                    pe.wait_ge(s["hid_done"], KH * (EX * c + e + 1))
                    if not (is_first(c) and e < 2):
                        pe.wait_ge(s["acc_done"], TQ * (EX * c + e - 1))
                    for t in range(TQ):
                        for k in range(KH):
                            last = t_.matmul(ob[e % 2][:, t * P:(t + 1) * P], hid[e % 2][:, k, t * P:(t + 1) * P],
                                             w3_s[:, e, k, :], start=k == 0, stop=k == KH - 1)
                    last.then_inc(s["down_done"], 1)

                def chunk(c):
                    for e in range(EX):
                        up(c, e)
                        if e > 0:
                            down(c, e - 1)
                        elif not is_first(c):
                            down(c - 1, EX - 1)
                chunk(0)
                with pe.Fori(1, NCH) as c:
                    chunk(c)
                down(NCH - 1, EX - 1)


_INS = ['x', 'Wq', 'bq', 'Wk', 'bk', 'Wv', 'bv', 'Wo', 'bo']
_FFN = ['ln1_scale', 'ln1_shift', 'wq', 'wk', 'wv', 'wo', 'bo', 'ln2_scale', 'ln2_shift', 'gate_w', 'w1', 'w2', 'w3']
_ALL = ['L0_attn_' + n for n in _INS] + ['L0_ffn_' + n for n in _FFN]


def kernel(**inputs):
    import numpy as _np
    import concourse.bacc as _bacc
    from concourse import mybir as _mybir
    from concourse.bass_utils import run_bass_kernel_spmd as _run

    nc = _bacc.Bacc("TRN2", target_bir_lowering=False, num_devices=1)
    arrays, args = {}, []
    for name in _ALL:
        a = _np.ascontiguousarray(inputs[name])
        arrays[f"in_{name}"] = a
        args.append(nc.dram_tensor(f"in_{name}", a.shape, _mybir.dt.from_np(a.dtype), kind="ExternalInput").ap())
    shape = inputs['L0_attn_x'].shape
    args.append(nc.dram_tensor("out_dram", shape, _mybir.dt.float32, kind="ExternalOutput").ap())
    preln_layer_kernel(nc, *args)
    r = _run(nc, [arrays], core_ids=[0])
    return r.results[0]["out_dram"]
```

```python
import concourse.bass as bass
from concourse import mybir
from contextlib import ExitStack
import math


def preln_layer_kernel(nc: bass.Bass, x, Wq, bq, Wk, bk, Wv, bv, Wo, bo,
                       ln1_scale, ln1_shift, wq, wk, wv, wo, fbo,
                       ln2_scale, ln2_shift, gate_w, w1, w2, w3, out):
    fp32 = mybir.dt.float32
    bf16 = mybir.dt.bfloat16
    fp32r = mybir.dt.float32r
    ALU = mybir.AluOpType
    ACT = mybir.ActivationFunctionType
    X = mybir.AxisListType.X

    P = 128
    B, S, D = x.shape
    NT = B * S // P
    H, HD = 16, 8
    EX, HID = w1.shape[0], w1.shape[2]
    EPS = 1e-5
    HG = 4
    NG = B * H // HG
    TB = S // P
    Q = 512
    SCALE = HD ** -0.5
    MASKED = -3.0e38
    KS = 96
    KM = 98
    PARTS = [(0, 0), (0, 1), (0, 2), (1, 0), (1, 1), (2, 0)]
    CH = 2
    NC = NT // CH
    W = CH * P

    def wait_alone(eng, semaphore, count):
        eng.wait_ge(semaphore, count)
        if not isinstance(count, int):
            eng.sem_inc(passed)

    def skewed(eng, fs, order=None, peeled=0):
        order = order or list(reversed(range(len(fs))))
        lag = len(fs) - 1
        peeled = max(peeled, lag, 2 + max(k for k in order if fs[k]))
        peeled += (NC - peeled) % 2

        def stages(i, parity):
            for k in order:
                if fs[k] and not (isinstance(i, int) and not 0 <= i - k < NC):
                    fs[k](i - k, (parity - k) % 2)
        for i in range(peeled):
            stages(i, i % 2)
        with eng.Fori(0, (NC - peeled) // 2) as n:
            for j in range(2):
                stages(2 * n + peeled + j, (peeled + j) % 2)
        for i in range(NC, NC + lag):
            stages(i, i % 2)

    def first(i, n=1):
        return isinstance(i, int) and i < n

    MAXU = []
    for c in (1, 0):
        for t in range(4 * c, TB):
            w = min(Q, (t + 1) * P - c * Q)
            n = {128: 4, 256: 2}.get(w, 1)
            MAXU += [(t, c, i, n, w) for i in range(0, HG, n)]
    EXPG = []
    for c in (1, 0):
        for j in range(4 * (c + 1)):
            w = (c + 1) * Q - max(c * Q, j * P)
            EXPG.append((c, j, w, j >= 4 * c))
    EXPU = [(n, i, {128: 4, 256: 2}.get(EXPG[n][2], 1)) for n in range(len(EXPG))
            for i in range(0, HG, {128: 4, 256: 2}.get(EXPG[n][2], 1))]
    NMU, NEU, NEG = len(MAXU), len(EXPU), len(EXPG)
    MASKED_ON_READ = [m for m, (t, c, i, n, w) in enumerate(MAXU) if n == 1 and t // 4 == c]
    LATE_UNITS = sum(1 for u in EXPU if EXPG[u[0]][0] == 1)
    LATE_KEYS = sum(1 for u in MAXU if u[1] == 1)
    NDG = sum(g[3] for g in EXPG)
    UNITS_UNTIL = [sum(1 for u in EXPU if u[0] <= n) for n in range(NEG)]
    DIAG_UNTIL = [sum(g[3] for g in EXPG[:n + 1]) for n in range(NEG)]

    def since(ring, u):
        before = [v for v in range(u) if ring[v] == ring[u]]
        if before:
            return before[-1] + 1
        return max(v for v in range(len(ring)) if ring[v] == ring[u]) + 1 - len(ring)


    PV_LAG = 2
    AHEAD = 2
    MAX_BY = 31
    AHEAD_FROM = 37

    def turn_order():
        order, m, e, turn_at = [], AHEAD, 0, NEG
        for n in range(NEG):
            if n == PV_LAG:
                order.append(("copy_ctx", 1))
            if n == 8 + PV_LAG:
                order.append(("copy_ctx", 0))
            for u in [u for u in EXPU if u[0] == n]:
                order.append(("exp", e))
                e += 1
                while m < min(NMU, AHEAD + -(-e * (NMU - AHEAD) // MAX_BY)):
                    order.append(("max", m))
                    m += 1
                if AHEAD_FROM <= e and m < NMU + AHEAD:
                    order.append(("max_ahead", m - NMU))
                    m += 1
            if m >= NMU and turn_at == NEG:
                order.append(("split_max", 0))
                turn_at = n + 1
            order.append(("pv", n - PV_LAG))
            if n == turn_at:
                order.append(("turn_max", 0))
            if n == PV_LAG + 1:
                order.append(("turn_ctx", 1))
            if n == NEG - 1:
                order.append(("turn_ctx", 0))
        for u in range(max(m - NMU, 0), AHEAD):
            order.append(("max_ahead", u))
        return order
    TURN = turn_order()
    EXPB = [e % 3 for e in range(NEU)]
    MAXB = [m % 3 for m in range(NMU)]

    ctx = ExitStack()
    with ctx:
        def sb(name, shape, dt=fp32):
            return ctx.enter_context(nc.sbuf_tensor(name, shape, dt))

        def sem(name):
            return ctx.enter_context(nc.semaphore(name))

        banks = [ctx.enter_context(nc.psum_tensor(f"bank{i}", [P, Q], fp32)) for i in range(8)]
        qparts = nc.dram_tensor("qparts", (2, B, 3, H // HG, HD, HG * Q), bf16, kind="Internal").ap()
        kparts = nc.dram_tensor("kparts", (2, B, 3, H // HG, HD, HG * Q), bf16, kind="Internal").ap()

        xs = sb("xs", [P, NT, D])
        yb = sb("yb", [P, NT, D])
        vs = sb("vs", [P, NT, D])
        att = sb("att", [P, NT, D])
        bn = sb("bn", [P, NT, 6])
        stats1 = sb("stats1", [P, NT, 2])
        rstd1 = sb("rstd1", [P, NT])
        ident = sb("ident", [P, P])
        identb = sb("identb", [P, P], bf16)
        headones = sb("headones", [P, P])
        maskb = sb("maskb", [P, P], bf16)
        hidden = sb("hidden", [P, Q])
        power = sb("power", [P, NT])
        Wq_s, Wk_s, Wv_s, Wo_s = (sb(n, [P, D]) for n in ("Wq_s", "Wk_s", "Wv_s", "Wo_s"))
        wq_s, wk_s, wv_s, wo_s = (sb(n, [P, D]) for n in ("wq_s", "wk_s", "wv_s", "wo_s"))
        cols = sb("cols", [P, 7])
        bq_c, bk_c, bv_c, s1_c, t1_c, s2_c, t2_c = (cols[:, i:i + 1] for i in range(7))
        bo_r = sb("bo_r", [P, D])
        fbo_r = sb("fbo_r", [P, D])

        w1_s = sb("w1_s", [P, EX, HID])
        w2_s = sb("w2_s", [P, EX, HID])
        w3_s = sb("w3_s", [P, EX, HID // P, D])
        gate_s = sb("gate_s", [P, EX])
        ffn_in = sem("ffn_weights_loaded")
        passed = sem("passed")
        w_in = sem("weights_loaded")
        consts = sem("consts_ready")

        operands = ctx.enter_context(ExitStack())
        NS = 2
        qop = [operands.enter_context(nc.sbuf_tensor(f"qop{i}", [P, 2, HG, Q], bf16)) for i in range(NS)]
        kop = [operands.enter_context(nc.sbuf_tensor(f"kop{i}", [P, 2, HG, Q], bf16)) for i in range(NS)]
        vop = [operands.enter_context(nc.sbuf_tensor(f"vop{i}", [P, TB, HG, 32], fp32)) for i in range(NS)]
        PAIR = Q // W
        STORED = 8
        qp, kp = (operands.enter_context(nc.sbuf_tensor(n, [P, STORED // PAIR, 3, PAIR * W], bf16))
                  for n in ("qp", "kp"))
        cleared = sem("operands_cleared")
        late_in = [sem(f"late_operands_loaded{i}") for i in range(NS)]
        early_in = [sem(f"early_operands_loaded{i}") for i in range(NS)]

        def load(eng, g, par, half):
            qrows, krows = (op[par][:, half].rearrange("p i t -> p (i t)") for op in (qop, kop))
            loaded = (late_in if half else early_in)[par]
            row = 0
            for part, times in ((0, 3), (1, 2), (2, 1)):
                rows = slice(row, row + times * HD)
                eng.dma_start(qrows[rows], qparts[half, g // 4, part, g % 4].unsqueeze(0)
                             .to_broadcast([times, HD, HG * Q])).then_inc(loaded, 16)
                eng.dma_start(krows[rows], kparts[half, g // 4, 0:times, g % 4]).then_inc(loaded, 16)
                row += times * HD

        with ExitStack() as mix, nc.Block() as block:
            def mb(name, shape, dt=fp32):
                return mix.enter_context(nc.sbuf_tensor(name, shape, dt))

            RING = 4
            EARLY = 2 * CH
            st0 = mb("st0", [P, NT, 2])
            ve0 = mb("ve0", [P, NT])
            rs0 = mb("rs0", [P, NT])
            h0 = [mb(f"h0_{i}", [P, CH, D]) for i in range(2)]
            h0T = [mb(f"h0T_{i}", [P, W]) for i in range(2)]
            sqa = [mb(f"sqa_{i}", [P, W]) for i in range(2)]
            sqb = [mb(f"sqb_{i}", [P, W]) for i in range(2)]
            sqs = [mb(f"sqs_{i}", [P, W]) for i in range(2)]
            eqk = [mb(f"eqk_{i}", [P, W]) for i in range(2)]
            ov = [mb(f"ov_{i}", [P, W]) for i in range(2)]
            ve1 = mb("ve1", [P, NT])
            ve2 = mb("ve2", [P, NT])
            rr = mb("rr", [P, NT])
            hh = [mb(f"hh_{i}", [P, CH, D]) for i in range(2)]
            hT = [mb(f"hT_{i}", [P, W]) for i in range(2)]
            wq_p = mb("wq_p", [P, D])
            wk_p = mb("wk_p", [P, D])
            qr = mb("qr", [P, RING, W])
            kr = mb("kr", [P, RING, W])

            def part_of(parts, i, n):
                return parts[:, i // PAIR % (STORED // PAIR), n, bass.ds(i % PAIR * W, W)]
            bT0, bAB, bO, bV, bC = banks[0:2], banks[2:4], banks[4:6], banks[6], banks[7]
            bT1, bQK, bV2 = banks[0:2], banks[2:4], banks[4:6]

            x_in = [sem(f"x_loaded{b}") for b in range(B)]
            names = ["bn0_done", "st0_done", "ve0_done", "rs0_done", "h0_done", "h0_turned", "h0T_done", "ab_done",
                     "vproj_done", "sq_done", "sqsum_done", "vb_done", "eqk_done", "coeff_done", "ov_done",
                     "wo_done", "xbo_done", "x1_done", "bn1_done", "st1_done", "ve1_done", "ve2_done", "rstd1_done",
                     "rr_done", "hh_done", "hh_turned", "hT_done", "qk_done", "v_done", "part1_done",
                     "rest_done", "part2_done", "part3_done", "vs_done", "qparts_stored", "kparts_stored", "order_done"]
            s = {n: sem(n) for n in names}
            parts_done, parts_stored = s["part3_done"], (s["qparts_stored"], s["kparts_stored"])
            parts_to = [a.rearrange("h b n g d (i t) -> h b (g d i) n t", i=HG) for a in (qparts, kparts)]

            def store(eng, j):
                wait_alone(eng, parts_done, 2 * PAIR * (j + 1))
                for parts, dst, stored in zip((qp, kp), parts_to, parts_stored):
                    if not first(j):
                        wait_alone(eng, stored, 16 * j)
                    eng.dma_start(dst[j % 2, j // 2], parts[:, j % (STORED // PAIR)]).then_inc(stored, 16)

            @block.sync
            def _(sp):
                xv = x.rearrange("b (t p) d -> b p t d", p=P)
                for b in range(B):
                    sp.dma_start(xs[:, b * TB:(b + 1) * TB, :], xv[b]).then_inc(x_in[b], 16)
                for dst, src in ((Wq_s, Wq), (Wk_s, Wk), (Wv_s, Wv), (Wo_s, Wo),
                                 (wq_s, wq), (wk_s, wk), (wv_s, wv), (wo_s, wo)):
                    sp.dma_start(dst[:, :], src).then_inc(w_in, 16)
                for dst, src in ((bq_c, bq), (bk_c, bk), (bv_c, bv), (s1_c, ln1_scale), (t1_c, ln1_shift),
                                 (s2_c, ln2_scale), (t2_c, ln2_shift)):
                    sp.dma_start(dst, src.rearrange("(p a) -> p a", a=1)).then_inc(w_in, 16)
                for dst, src in ((bo_r, bo), (fbo_r, fbo)):
                    sp.dma_start(dst[:, :], src.partition_broadcast(P)).then_inc(w_in, 16)
                store(sp, 0)
                with sp.Fori(1, NC // PAIR - 2) as j:
                    store(sp, j)
                sp.wait_ge(cleared, 5 * NS)
                load(sp, 0, 0, 1)
                load(sp, 0, 0, 0)

            @block.gpsimd
            def _(pool):
                g = nc.gpsimd
                g.memset(power[:, :], -0.5).then_inc(consts, 1)
                g.memset(ident[:, :], 0.0).then_inc(consts, 1)
                g.memset(headones[:, :], 1.0).then_inc(consts, 1)
                g.memset(maskb[:, :], 0.0).then_inc(consts, 1)
                g.memset(hidden[:, :], 0.0).then_inc(consts, 1)
                pool.wait_ge(consts, 5)
                g.affine_select(out=ident[:, :], in_=ident[:, :], compare_op=ALU.not_equal, fill=1.0,
                                base=0, pattern=[[-1, P]], channel_multiplier=1).then_inc(consts, 1)
                hv = headones[:, :].rearrange("p (h d) -> p h d", d=HD)
                g.affine_select(out=hv, in_=hv, compare_op=ALU.is_ge, fill=0.0, base=0,
                                pattern=[[-HD, H], [0, HD]], channel_multiplier=1).then_inc(consts, 1)
                g.affine_select(out=maskb[:, :], in_=maskb[:, :], compare_op=ALU.is_ge, fill=MASKED,
                                base=0, pattern=[[-1, P]], channel_multiplier=1).then_inc(consts, 1)
                g.affine_select(out=hidden[:, Q - P:Q], in_=hidden[:, Q - P:Q], compare_op=ALU.is_ge, fill=MASKED,
                                base=0, pattern=[[-1, P]], channel_multiplier=1).then_inc(consts, 1)
                pool.wait_ge(consts, 9)
                g.affine_select(out=hv, in_=hv, compare_op=ALU.is_ge, fill=0.0, base=HD - 1,
                                pattern=[[HD, H], [0, HD]], channel_multiplier=-1).then_inc(consts, 1)
                g.tensor_copy(identb[:, :], ident[:, :]).then_inc(consts, 1)
                pool.wait_ge(s["ve0_done"], 1)
                for c in (slice(0, EARLY), slice(EARLY, NT)):
                    g.tensor_tensor(rs0[:, c], ve0[:, c], power[:, c], ALU.pow).then_inc(s["rs0_done"], 1)
                for i in range(NS):
                    g.memset(vop[i][:, :, :, :], 0.0).then_inc(cleared, 1)
                pool.wait_ge(cleared, 3 * NS)
                for i in range(NS):
                    g.memset(kop[i][KS:KM, :, :, :], -1.0).then_inc(cleared, 1)
                pool.wait_ge(cleared, 4 * NS)
                for i in range(NS):
                    g.memset(vop[i][:, :, :, HD:HD + 1], 1.0).then_inc(cleared, 1)
                pool.wait_ge(w_in, 16 * 17)

                def add_bias(i, par):
                    wait_alone(pool, s["h0_done"], CH * (i + 1))
                    xc = xs[:, bass.ds(CH * i, CH), :]
                    g.tensor_tensor(xc, xc, bo_r[:, :].unsqueeze(1).to_broadcast([P, CH, D]), ALU.add)\
                        .then_inc(s["xbo_done"], 1)
                skewed(pool, [None, add_bias, None, None, None, None, None])
                pool.wait_ge(s["ve2_done"], 1)
                for c in (slice(0, EARLY), slice(EARLY, NT)):
                    g.tensor_tensor(rr[:, c], ve2[:, c], power[:, c], ALU.pow).then_inc(s["rr_done"], 1)
                pool.wait_ge(s["ve1_done"], 1)
                g.tensor_tensor(rstd1[:, :], ve1[:, :], power[:, :], ALU.pow).then_inc(s["rstd1_done"], 1)

                def part3(i, par):
                    for n, (parts, rest) in enumerate(((qp, qr), (kp, kr))):
                        wait_alone(pool, s["part2_done"], 2 * i + n + 1)
                        g.tensor_tensor(part_of(parts, i, 2), rest[:, i % RING, :], part_of(parts, i, 1),
                                        ALU.subtract).then_inc(s["part3_done"], 1)
                skewed(pool, [None, None, None, None, part3])

            @block.vector
            def _(dve):
                v = nc.vector
                v.memset(kop[0][:, :, :, :], 0.0).then_inc(cleared, 1)
                v.memset(qop[0][:, :, :, :], 0.0).then_inc(cleared, 1)
                for b in range(B):
                    dve.wait_ge(x_in[b], 16)
                    for t in range(b * TB, (b + 1) * TB):
                        v.bn_stats(bn[:, t, :], xs[:, t, :]).then_inc(s["bn0_done"], 1)
                dve.wait_ge(s["bn0_done"], NT)
                for t in range(NT):
                    v.bn_aggr(st0[:, t, :], bn[:, t, :]).then_inc(s["st0_done"], 1)
                dve.wait_ge(s["st0_done"], NT)
                v.tensor_scalar(ve0[:, :], st0[:, :, 1], EPS, None, ALU.add).then_inc(s["ve0_done"], 1)
                v.memset(kop[1][:, :, :, :], 0.0).then_inc(cleared, 1)
                v.memset(qop[1][:, :, :, :], 0.0).then_inc(cleared, 1)

                def norm_x(i, par):
                    dve.wait_ge(s["rs0_done"], 1 if first(i, EARLY // CH) else 2)
                    if not first(i, 2):
                        dve.wait_ge(s["h0_turned"], i - 1)
                    for t in range(CH):
                        v.tensor_scalar(h0[par][:, t, :], xs[:, CH * i + t, :], st0[:, CH * i + t, 0:1],
                                        rs0[:, bass.ds(CH * i + t, 1)], ALU.subtract, ALU.mult)\
                            .then_inc(s["h0_done"], 1)

                def square_sum(i, par):
                    dve.wait_ge(s["sq_done"], 2 * i + 2)
                    if not first(i, 2):
                        dve.wait_ge(s["eqk_done"], i - 1)
                    v.tensor_tensor(sqs[par][:, :], sqa[par][:, :], sqb[par][:, :], ALU.add).then_inc(s["sqsum_done"], 1)

                def mix(i, par):
                    dve.wait_ge(s["coeff_done"], i + 1)
                    dve.wait_ge(s["vb_done"], i + 1)
                    if not first(i, 2):
                        dve.wait_ge(s["wo_done"], i - 1)
                    vb = att[:, bass.ds(CH * i, CH), :].rearrange("p t d -> p (t d)")
                    v.tensor_tensor(ov[par][:, :], bC[:, 0:W], vb, ALU.mult).then_inc(s["ov_done"], 1)

                def make_x1(i, par):
                    dve.wait_ge(s["wo_done"], i + 1)
                    dve.wait_ge(s["xbo_done"], i + 1)
                    x1 = xs[:, bass.ds(CH * i, CH), :]
                    v.tensor_tensor(x1, bO[par][:, 0:W].rearrange("p (t d) -> p t d", t=CH), x1,
                                    ALU.add).then_inc(s["x1_done"], 1)

                def x1_stats(i, par):
                    wait_alone(dve, s["x1_done"], i + 1)
                    for t in range(CH):
                        v.bn_stats(bn[:, CH * i + t, :], xs[:, CH * i + t, :]).then_inc(s["bn1_done"], 1)
                skewed(dve, [norm_x, None, None, square_sum, mix, make_x1, x1_stats], [3, 5, 4, 0, 6])
                dve.wait_ge(s["bn1_done"], NT)
                for t in range(NT):
                    v.bn_aggr(stats1[:, t, :], bn[:, t, :]).then_inc(s["st1_done"], 1)
                dve.wait_ge(s["st1_done"], NT)
                var = stats1[:, :, 1]
                v.tensor_scalar(ve2[:, :], var, 1.0 + EPS, EPS * EPS, ALU.mult, ALU.add).then_inc(s["ve2_done"], 1)
                v.tensor_scalar(ve1[:, :], var, EPS, None, ALU.add).then_inc(s["ve1_done"], 1)

                def norm_x1(i, par):
                    dve.wait_ge(s["rr_done"], 1 if first(i, EARLY // CH) else 2)
                    if not first(i, 2):
                        dve.wait_ge(s["hh_turned"], i - 1)
                    for t in range(CH):
                        v.tensor_scalar(hh[par][:, t, :], xs[:, CH * i + t, :], stats1[:, CH * i + t, 0:1],
                                        rr[:, bass.ds(CH * i + t, 1)], ALU.subtract, ALU.mult)\
                            .then_inc(s["hh_done"], 1)

                def rests(i, par):
                    dve.wait_ge(s["part1_done"], 2 * i + 2)
                    for n, (parts, rest) in enumerate(((qp, qr), (kp, kr))):
                        if not first(i, RING):
                            dve.wait_ge(s["part3_done"], 2 * (i - RING) + n + 1)
                        v.tensor_tensor(rest[:, i % RING, :], bQK[par][:, n * W:(n + 1) * W], part_of(parts, i, 0),
                                        ALU.subtract).then_inc(s["rest_done"], 1)

                def part2(i, par):
                    for n, (parts, rest) in enumerate(((qp, qr), (kp, kr))):
                        dve.wait_ge(s["rest_done"], 2 * i + n + 1)
                        v.tensor_copy(part_of(parts, i, 1), rest[:, i % RING, :]).then_inc(s["part2_done"], 1)
                skewed(dve, [norm_x1, None, None, rests, part2], [0, 3, 4], peeled=RING + 3)

            @block.scalar
            def _(act):
                a = nc.scalar
                act.wait_ge(w_in, 16 * 17)
                for dst, src in ((wq_p, wq_s), (wk_p, wk_s)):
                    a.copy(dst[:, :].rearrange("p (g d i) -> p g d i", d=HD, i=HG),
                           src[:, :].rearrange("p (g i d) -> p g d i", d=HD, i=HG)).then_inc(s["order_done"], 1)

                def turned(i, par):
                    act.wait_ge(s["h0_turned"], i + 1)
                    if not first(i, 2):
                        act.wait_ge(s["vproj_done"], i - 1)
                    a.copy(h0T[par][:, :], bT0[par][:, 0:W]).then_inc(s["h0T_done"], 1)

                def squares(i, par):
                    act.wait_ge(s["ab_done"], i + 1)
                    if not first(i, 2):
                        act.wait_ge(s["sqsum_done"], i - 1)
                    a.activation(sqa[par][:, :], bAB[par][:, 0:W], ACT.Square, bias=bq_c).then_inc(s["sq_done"], 1)
                    a.activation(sqb[par][:, :], bAB[par][:, W:2 * W], ACT.Square, bias=bk_c).then_inc(s["sq_done"], 1)
                    act.wait_ge(s["vproj_done"], i + 1)
                    vb = att[:, bass.ds(CH * i, CH), :].rearrange("p t d -> p (t d)")
                    a.activation(vb, bV[:, 0:W], ACT.Identity, bias=bv_c).then_inc(s["vb_done"], 1)

                def exponential(i, par):
                    act.wait_ge(s["sqsum_done"], i + 1)
                    if not first(i, 2):
                        act.wait_ge(s["coeff_done"], i - 1)
                    a.activation(eqk[par][:, :], sqs[par][:, :], ACT.Exp, scale=-0.5).then_inc(s["eqk_done"], 1)
                skewed(act, [None, turned, squares, exponential, None, None, None])

                def scale_shift(i, par):
                    act.wait_ge(s["hh_turned"], i + 1)
                    if not first(i, 2):
                        act.wait_ge(s["v_done"], i - 1)
                    a.activation(hT[par][:, :], bT1[par][:, 0:W], ACT.Identity, bias=t1_c, scale=s1_c).then_inc(s["hT_done"], 1)

                def part1(i, par):
                    act.wait_ge(s["qk_done"], i + 1)
                    for n, (parts, stored) in enumerate(((qp, s["qparts_stored"]), (kp, s["kparts_stored"]))):
                        if not first(i, STORED):
                            act.wait_ge(stored, 16 * ((i - STORED) // PAIR + 1))
                        a.copy(part_of(parts, i, 0), bQK[par][:, n * W:(n + 1) * W]).then_inc(s["part1_done"], 1)
                    act.wait_ge(s["v_done"], i + 1)
                    a.copy(vs[:, bass.ds(CH * i, CH), :], bV2[par][:, 0:W].rearrange("p (t d) -> p t d", t=CH))\
                        .then_inc(s["vs_done"], 1)
                skewed(act, [None, scale_shift, part1, None, None], [1, 2], peeled=STORED + 2)

            @block.tensor
            def _(pe):
                t_ = nc.tensor
                pe.wait_ge(consts, 11)
                pe.wait_ge(w_in, 16 * 17)
                pe.wait_ge(s["order_done"], 2)

                def turn(i, par):
                    pe.wait_ge(s["h0_done"], CH * (i + 1))
                    if not first(i, 2):
                        pe.wait_ge(s["h0T_done"], i - 1)
                    for t in range(CH):
                        last = t_.transpose(bT0[par][:, t * P:(t + 1) * P], h0[par][:, t, :], ident[:, :])
                    last.then_inc(s["h0_turned"], 1)

                def project(i, par):
                    pe.wait_ge(s["h0T_done"], i + 1)
                    if not first(i, 2):
                        pe.wait_ge(s["sq_done"], 2 * (i - 1))
                    t_.matmul(bAB[par][:, 0:W], Wq_s[:, :], h0T[par][:, :], start=True, stop=True)
                    t_.matmul(bAB[par][:, W:2 * W], Wk_s[:, :], h0T[par][:, :], start=True, stop=True).then_inc(s["ab_done"], 1)
                    if not first(i):
                        pe.wait_ge(s["vb_done"], i)
                    t_.matmul(bV[:, 0:W], Wv_s[:, :], h0T[par][:, :], start=True, stop=True).then_inc(s["vproj_done"], 1)

                def coeff(i, par):
                    pe.wait_ge(s["eqk_done"], i + 1)
                    if not first(i):
                        pe.wait_ge(s["ov_done"], i)
                    t_.matmul(bC[:, 0:W], headones[:, :], eqk[par][:, :], start=True, stop=True).then_inc(s["coeff_done"], 1)

                def mix_out(i, par):
                    pe.wait_ge(s["ov_done"], i + 1)
                    if not first(i, 2):
                        pe.wait_ge(s["x1_done"], i - 1)
                    for t in range(CH):
                        last = t_.matmul(bO[par][:, t * P:(t + 1) * P], ov[par][:, t * P:(t + 1) * P], Wo_s[:, :],
                                         start=True, stop=True)
                    last.then_inc(s["wo_done"], 1)
                skewed(pe, [None, turn, project, None, coeff, mix_out, None])

                def turn2(i, par):
                    pe.wait_ge(s["hh_done"], CH * (i + 1))
                    if not first(i, 2):
                        pe.wait_ge(s["hT_done"], i - 1)
                    for t in range(CH):
                        last = t_.transpose(bT1[par][:, t * P:(t + 1) * P], hh[par][:, t, :], ident[:, :])
                    last.then_inc(s["hh_turned"], 1)

                def heads(i, par):
                    pe.wait_ge(s["hT_done"], i + 1)
                    if not first(i, 2):
                        pe.wait_ge(s["rest_done"], 2 * (i - 1))
                    t_.matmul(bQK[par][:, 0:W], wq_p[:, :], hT[par][:, :], start=True, stop=True)
                    t_.matmul(bQK[par][:, W:2 * W], wk_p[:, :], hT[par][:, :], start=True, stop=True).then_inc(s["qk_done"], 1)
                    if not first(i, 2):
                        pe.wait_ge(s["vs_done"], i - 1)
                    for t in range(CH):
                        last = t_.matmul(bV2[par][:, t * P:(t + 1) * P], hT[par][:, t * P:(t + 1) * P], wv_s[:, :],
                                         start=True, stop=True)
                    last.then_inc(s["v_done"], 1)
                skewed(pe, [None, turn2, heads, None, None], [1, 2])

        with ExitStack() as at, nc.Block() as block:
            def ab(name, shape, dt=fp32):
                return at.enter_context(nc.sbuf_tensor(name, shape, dt))

            NB = 4
            probs = [ab(f"probs{i}", [P, HG, Q]) for i in range(NB)]
            rowmax = ab("rowmax", [P, 2, HG, TB // 2])
            latemax = ab("latemax", [P, HG, TB // 2])
            maxparts = ab("maxparts", [P, 2, 2, HG, TB // 2], bf16)
            maxrows = ab("maxrows", [2 * HG * TB, P], bf16)
            ctxT = ab("ctxT", [P, Q])
            recip = ab("recip", [P, 4, HG])
            unread = ab("unread", [P, 2, Q])
            centred = ab("centred", [P, CH, D])
            scaled = ab("scaled", [P, CH, D])
            expb, maxb, pvb, miscb = banks[0:3], banks[3:6], banks[6], banks[7]

            rows_in = [sem(f"maxrows_loaded{i}") for i in range(NS)]
            names = ["st_done", "exp_done", "select_done", "vop_ready", "pv_done",
                     "ctx_out", "ctx_turned", "recip_done", "ctx_done", "max_done", "maxred_done", "rowmax_done",
                     "maxhi_done", "maxlo_done", "max_turned", "maxrows_out", "residual_step"]
            s = {n: sem(n) for n in names}

            def turns(eng, body):
                body(0, 0, 0)
                with eng.Fori(0, NG // 2 - 2) as p:
                    body(2 * p + 1, p, 1)
                    body(2 * p + 2, p + 1, 0)
                for g in range(NG - 3, NG):
                    body(g, g // 2, g % 2)

            def is_first(g):
                return isinstance(g, int) and g == 0

            def is_last(g):
                return isinstance(g, int) and g == NG - 1

            def has_two_after(g):
                return not (isinstance(g, int) and g + 2 >= NG)

            def nxt(g, k, par):
                return g + 1, (k if par < NS - 1 else k + 1), (par + 1) % NS

            @block.sync
            def _(sp):
                def max_rows(g, k, par):
                    sp.wait_ge(s["maxrows_out"], g + 1)
                    sp.dma_start(qop[par][KS:KM].rearrange("p h i q -> p (h i q)"), maxrows[:, :])\
                        .then_inc(rows_in[par], 16)
                store(sp, NC // PAIR - 2)
                load(sp, 1, 1, 1)
                store(sp, NC // PAIR - 1)
                load(sp, 1, 1, 0)
                max_rows(0, 0, 0)

                sp.dma_start(gate_s[:, :], gate_w).then_inc(ffn_in, 16)
                sp.dma_start(w1_s[:, :, :], w1.rearrange("e d h -> d e h")).then_inc(ffn_in, 16)
                sp.dma_start(w2_s[:, :, :], w2.rearrange("e d h -> d e h")).then_inc(ffn_in, 16)
                for k in range(HID // P):
                    sp.dma_start(w3_s[:, :, k, :], w3[:, k * P:(k + 1) * P, :].rearrange("e h d -> h e d"))\
                        .then_inc(ffn_in, 16)

                def turn(g, k, par):
                    more = has_two_after(g)
                    if more:
                        wait_alone(sp, s["st_done"], NEU * g + LATE_UNITS)
                        load(sp, g + 2, par, 1)
                    if not is_last(g):
                        max_rows(*nxt(g, k, par))
                    if is_first(g):
                        for stored in parts_stored:
                            sp.wait_ge(stored, 16 * NC // PAIR)
                    if more:
                        wait_alone(sp, s["st_done"], NEU * (g + 1))
                        load(sp, g + 2, par, 0)
                turns(sp, turn)

            @block.gpsimd
            def _(pool):
                g_ = nc.gpsimd
                def vcopy(g, k, par):
                    if not (isinstance(g, int) and g < 2):
                        wait_alone(pool, s["pv_done"], NEG * (g - 1))
                    src = vs[:, bass.ds((g // 4) * TB, TB), bass.ds((g % 4) * HG * HD, HG * HD)]
                    g_.tensor_copy(vop[par][:, :, :, 0:HD], src.rearrange("p t (i d) -> p t i d", d=HD))\
                        .then_inc(s["vop_ready"], 1)
                vcopy(0, 0, 0)

                def residual(g, step):
                    xc, yc = (a[:, bass.ds(CH * g, CH), :] for a in (xs, yb))
                    mean = stats1[:, bass.ds(CH * g, CH), 0:1].to_broadcast([P, CH, D])
                    rstd = rstd1[:, bass.ds(CH * g, CH)].unsqueeze(2).to_broadcast([P, CH, D])
                    bias = fbo_r[:, :].unsqueeze(1).to_broadcast([P, CH, D])
                    out, a, b, op = ((centred[:, :, :], xc, mean, ALU.subtract),
                                     (scaled[:, :, :], centred[:, :, :], rstd, ALU.mult),
                                     (yc, scaled[:, :, :], bias, ALU.add),
                                     (xc, xc, yc, ALU.add))[step]
                    if not (is_first(g) and step == 0):
                        wait_alone(pool, s["residual_step"], 4 * g + step)
                    g_.tensor_tensor(out, a, b, op).then_inc(s["residual_step"], 1)

                def turn(g, k, par):
                    for n in range(NEG):
                        if n < 4:
                            residual(g, n)
                        if EXPG[n][3]:
                            wait_alone(pool, s["exp_done"], NEU * g + UNITS_UNTIL[n])
                            d = probs[n % NB][:, :, 0:P]
                            g_.affine_select(out=d, in_=d, compare_op=ALU.is_ge, fill=0.0, base=0,
                                             pattern=[[0, HG], [1, P]], channel_multiplier=-1)\
                                .then_inc(s["select_done"], 1)
                        if n == 6 and not is_last(g):
                            vcopy(*nxt(g, k, par))
                turns(pool, turn)

            @block.vector
            def _(dve):
                v = nc.vector
                def max_unit(g, m):
                    t, c, i, n, w = MAXU[m]
                    if m in MASKED_ON_READ:
                        wait_alone(dve, s["max_done"], NMU * g + m + 1)
                    else:
                        dve.wait_ge(s["max_done"], NMU * g + m + 1)
                    dst = rowmax[:, t // 4, i:i + n, t % 4:t % 4 + 1] if c == 0 else latemax[:, i:i + n, t - 4:t - 3]
                    if m in MASKED_ON_READ:
                        j = MASKED_ON_READ.index(m)
                        if not (is_first(g) and j < 2):
                            before = MASKED_ON_READ[j - 2] - (NMU if j < 2 else 0)
                            wait_alone(dve, s["maxred_done"], NMU * g + before + 1)
                        v.tensor_tensor_reduce(out=unread[:, j % 2, 0:w], in0=maxb[MAXB[m]][:, 0:w],
                                               in1=hidden[:, Q - w:Q], scale=1.0, scalar=MASKED,
                                               op0=ALU.add, op1=ALU.max, accum_out=dst[:, 0, :])\
                            .then_inc(s["maxred_done"], 1)
                        return
                    src = maxb[MAXB[m]][:, 0:n * w].rearrange("p (i k) -> p i k", i=n)
                    v.tensor_reduce(dst, src, X, ALU.max).then_inc(s["maxred_done"], 1)

                def row_max(g):
                    dve.wait_ge(s["maxred_done"], NMU * (g + 1))
                    late = rowmax[:, 1, :, :]
                    v.tensor_tensor(late, late, latemax[:, :, :], ALU.max).then_inc(s["rowmax_done"], 1)
                    dve.wait_ge(s["rowmax_done"], g + 1)
                    if not is_first(g):
                        dve.wait_ge(s["max_turned"], g)
                    v.tensor_copy(maxparts[:, 0], rowmax[:, :, :, :]).then_inc(s["maxhi_done"], 1)
                    dve.wait_ge(s["maxhi_done"], g + 1)
                    v.tensor_tensor(maxparts[:, 1], rowmax[:, :, :, :], maxparts[:, 0], ALU.subtract)\
                        .then_inc(s["maxlo_done"], 1)

                def max_rows_out(g):
                    dve.wait_ge(s["max_turned"], g + 1)
                    if not is_first(g):
                        dve.wait_ge(*rows_before(g))
                    v.tensor_copy(maxrows[:, :], miscb[0:2 * HG * TB, 0:P // 2].bitcast(bf16))\
                        .then_inc(s["maxrows_out"], 1)

                par_of = {}

                def rows_before(g):
                    par, k = par_of["now"]
                    return rows_in[(par - 1) % NS], 16 * (k if par == 0 else k + 1)

                def normalize(g, half):
                    dve.wait_ge(s["ctx_turned"], 2 * g + half + 1)
                    cv = miscb[:, :].rearrange("p (t i c) -> p t i c", t=4, i=HG)
                    v.reciprocal(recip[:, :, :], cv[:, :, :, HD]).then_inc(s["recip_done"], 1)
                    dve.wait_ge(s["recip_done"], 2 * g + half + 1)
                    first_tile = (g // 4) * TB + (4 if half == 0 else 0)
                    dst = att[:, bass.ds(first_tile, 4), bass.ds((g % 4) * HG * HD, HG * HD)]
                    v.tensor_tensor(dst.rearrange("p t (i d) -> p t i d", d=HD), cv[:, :, :, 0:HD],
                                    recip[:, :, :].unsqueeze(3).to_broadcast([P, 4, HG, HD]), ALU.mult)\
                        .then_inc(s["ctx_done"], 1)

                par_of["now"] = (0, 0)
                for m in range(NMU):
                    max_unit(0, m)
                row_max(0)
                max_rows_out(0)
                for m in range(AHEAD):
                    max_unit(1, m)

                def turn(g, k, par):
                    for what, m in TURN:
                        if what == "max" and not is_last(g):
                            max_unit(g + 1, m)
                        if what == "max_ahead" and has_two_after(g):
                            max_unit(g + 2, m)
                        if what == "split_max" and not is_last(g):
                            row_max(g + 1)
                        if what == "turn_max" and not is_last(g):
                            g1, k1, par1 = nxt(g, k, par)
                            par_of["now"] = (par1, k1)
                            max_rows_out(g1)
                        if what == "turn_ctx" and m == 1 and not is_first(g):
                            normalize(g - 1, 1)
                        if what == "turn_ctx" and m == 0:
                            normalize(g, 0)
                turns(dve, turn)
                normalize(NG - 1, 1)

            @block.scalar
            def _(act):
                a = nc.scalar

                def exp_unit(g, e):
                    n, i, heads = EXPU[e]
                    w = EXPG[n][2]
                    if i == 0 and not (is_first(g) and n < NB):
                        act.wait_ge(s["pv_done"], NEG * g + n - NB + 1)
                    act.wait_ge(s["st_done"], NEU * g + e + 1)
                    a.activation(probs[n % NB][:, i:i + heads, 0:w],
                                 expb[EXPB[e]][:, 0:heads * w].rearrange("p (i q) -> p i q", i=heads),
                                 ACT.Exp, scale=SCALE).then_inc(s["exp_done"], 1)

                def ctx_copy(g, half):
                    act.wait_ge(s["pv_done"], NEG * g + (8 if half == 0 else 12))
                    if not (is_first(g) and half == 0):
                        act.wait_ge(s["ctx_turned"], 2 * g + half)
                    a.copy(ctxT[:, :], pvb[:, :]).then_inc(s["ctx_out"], 1)

                def turn(g, k, par):
                    for what, m in TURN:
                        if what == "exp":
                            exp_unit(g, m)
                        if what == "copy_ctx" and m == 1 and not is_first(g):
                            ctx_copy(g - 1, 1)
                        if what == "copy_ctx" and m == 0:
                            ctx_copy(g, 0)
                turns(act, turn)
                ctx_copy(NG - 1, 1)

            @block.tensor
            def _(pe):
                t_ = nc.tensor

                def max_unit(g, k, par, m):
                    t, c, i, n, w = MAXU[m]
                    if m == 0:
                        pe.wait_ge(late_in[par], LOADS * (k + 1))
                    if m == LATE_KEYS:
                        pe.wait_ge(early_in[par], LOADS * (k + 1))
                    if not (is_first(g) and m < 3):
                        pe.wait_ge(s["maxred_done"], NMU * g + since(MAXB, m))
                    diag = t // 4 == c and m not in MASKED_ON_READ
                    for h in range(n):
                        o = maxb[MAXB[m]][:, h * w:(h + 1) * w]
                        last = t_.matmul(o, qop[par][0:KS, t // 4, i + h, t % 4 * P:(t % 4 + 1) * P],
                                         kop[par][0:KS, c, i + h, 0:w], start=True, stop=not diag)
                        if diag:
                            last = t_.matmul(o[:, w - P:w], identb[:, :], maskb[:, :], start=False, stop=True)
                    last.then_inc(s["max_done"], 1)

                def st_unit(g, par, e):
                    n, i, heads = EXPU[e]
                    c, j, w, _ = EXPG[n]
                    if not (is_first(g) and e < 3):
                        pe.wait_ge(s["exp_done"], NEU * g + since(EXPB, e))
                    for h in range(heads):
                        last = t_.matmul(expb[EXPB[e]][:, h * w:(h + 1) * w], 
                                         kop[par][0:KM, j // 4, i + h, j % 4 * P:(j % 4 + 1) * P],
                                         qop[par][0:KM, c, i + h, Q - w:Q], start=True, stop=True)
                    last.then_inc(s["st_done"], 1)

                def pv_group(g, par, n):
                    c, j, w, diag = EXPG[n]
                    if n == 0:
                        pe.wait_ge(s["vop_ready"], g + 1)
                        if not is_first(g):
                            pe.wait_ge(s["ctx_out"], 2 * g)
                    if n == 8:
                        pe.wait_ge(s["ctx_out"], 2 * g + 1)
                    pe.wait_ge(s["exp_done"], NEU * g + UNITS_UNTIL[n])
                    if diag:
                        pe.wait_ge(s["select_done"], NDG * g + DIAG_UNTIL[n])
                    for i in range(HG):
                        last = t_.matmul(pvb[32 * i:32 * i + 32, Q - w:Q], vop[par][:, j, i, :],
                                         probs[n % NB][:, i, 0:w], start=j == 0, stop=j == 4 * c + 3)
                    last.then_inc(s["pv_done"], 1)

                def turn_ctx(g, half):
                    pe.wait_ge(s["ctx_out"], 2 * g + half + 1)
                    if half == 1:
                        pe.wait_ge(s["ctx_done"], 2 * g + 1)
                    elif is_last(g):
                        pe.wait_ge(s["ctx_done"], 2 * g)
                    else:
                        pe.wait_ge(s["maxrows_out"], g + 2)
                    for t in range(4):
                        last = t_.transpose(miscb[:, t * P:(t + 1) * P], ctxT[:, t * P:(t + 1) * P], ident[:, :])
                    last.then_inc(s["ctx_turned"], 1)

                def turn_max(g):
                    wait_alone(pe, s["maxlo_done"], g + 1)
                    if isinstance(g, int) and g == 1:
                        pe.wait_ge(s["maxrows_out"], 1)
                    elif not is_first(g):
                        wait_alone(pe, s["ctx_done"], 2 * g - 2)
                    t_.transpose(miscb[0:2 * HG * TB, 0:P // 2].bitcast(bf16),
                                 maxparts[:, :, :, :, :].rearrange("p a h i t -> p (a h i t)"), identb[:, :])\
                        .then_inc(s["max_turned"], 1)

                LOADS = 6 * 16
                for m in range(NMU):
                    max_unit(0, 0, 0, m)
                turn_max(0)
                for m in range(AHEAD):
                    max_unit(1, 0, 1, m)

                def turn(g, k, par):
                    g1, k1, par1 = nxt(g, k, par)
                    pe.wait_ge(rows_in[par], 16 * (k + 1))
                    for what, m in TURN:
                        if what == "exp":
                            st_unit(g, par, m)
                        if what == "max" and not is_last(g):
                            max_unit(g1, k1, par1, m)
                        if what == "max_ahead" and has_two_after(g):
                            max_unit(*nxt(g1, k1, par1), m)
                        if what == "pv" and m >= 0:
                            pv_group(g, par, m)
                        if what == "pv" and m < 0 and not is_first(g):
                            pv_group(g - 1, (par - 1) % NS, NEG + m)
                        if what == "turn_ctx" and m == 1 and not is_first(g):
                            turn_ctx(g - 1, 1)
                        if what == "turn_ctx" and m == 0:
                            turn_ctx(g, 0)
                        if what == "turn_max" and not is_last(g):
                            turn_max(g1)
                turns(pe, turn)
                for n in range(NEG - PV_LAG, NEG):
                    pv_group(NG - 1, (NG - 1) % NS, n)
                turn_ctx(NG - 1, 1)

        operands.close()

        with ExitStack() as ff, nc.Block() as block:
            def eb(name, shape, dt=fp32):
                return ff.enter_context(nc.sbuf_tensor(name, shape, dt))

            NCH = NT * P // Q
            TQ = Q // P
            KH = HID // P
            NU = EX * KH
            h2_head = eb("h2_head", [P, NT * P])
            h2_rest = eb("h2_rest", [P, NT * P])
            w1_head = eb("w1_head", [P, EX, HID])
            w2_head = eb("w2_head", [P, EX, HID])
            w1_rest = eb("w1_rest", [P, EX, HID])
            w2_rest = eb("w2_rest", [P, EX, HID])
            attc = eb("attc", [P, TQ, D])
            attT = eb("attT", [P, Q])
            z = eb("z", [P, TQ, D])
            bnz = eb("bnz", [P, TQ, 6])
            stz = eb("stz", [P, TQ, 2])
            vez = eb("vez", [P, TQ])
            rstdz = eb("rstdz", [P, TQ])
            hz = eb("hz", [P, TQ, D])
            hzT = eb("hzT", [P, Q])
            rank = eb("rank", [P, EX])
            logits, sel, oh1, oh2, rest = (eb(n, [P, TQ, EX]) for n in ("logits", "sel", "oh1", "oh2", "rest"))
            euler = eb("euler", [P, TQ])
            best = eb("best", [P, 2, TQ])
            pick, gap, egap, eone = (eb(n, [P, TQ]) for n in ("pick", "gap", "egap", "eone"))
            pr = eb("pr", [P, 2, TQ])
            wc = eb("wc", [P, TQ, EX])
            silu = [eb(f"silu{i}", [P, Q]) for i in range(2)]
            hid = [eb(f"hid{i}", [P, KH, Q]) for i in range(2)]
            base = eb("base", [P, TQ, D])
            acc = eb("acc", [P, TQ, D])
            outb = eb("outb", [P, TQ, D])
            gb, ub, ob, pA, pB = banks[0:2], banks[2:4], banks[4:6], banks[6], banks[7]
            names = ["rank_done", "w_head_done", "w_rest_done", "attc_done", "att_turned", "attT_done", "wo2_done",
                     "z_done", "resid_done", "bnz_done", "stz_done", "vez_done", "rstdz_done", "hz_done", "hz_turned",
                     "hzT_done", "head_done", "h2T_done", "gate_done", "logits_done", "gating_step", "gap_done",
                     "egap_done", "wc_done",
                     "up_done", "silu_done", "hid_done", "down_done", "acc_done", "base_ready", "out_stored"]
            s = {n: sem(n) for n in names}

            def is_first(c):
                return isinstance(c, int) and c == 0

            def is_last(c):
                return isinstance(c, int) and c == NCH - 1

            def chunks(body):
                def run(eng):
                    body(0)
                    with eng.Fori(1, NCH - 1) as c:
                        body(c)
                    body(NCH - 1)
                return run

            def prepare(prep, c, u):
                for f in prep.get(NU + u, ()):
                    f(c)
                if u in prep and not is_last(c):
                    for f in prep[u]:
                        f(c + 1)

            def prepare_all(prep, p):
                for u in range(NU):
                    for f in prep.get(u, ()):
                        f(p)

            @block.sync
            def _(sp):
                ov = out.rearrange("b s d -> (b s) d").rearrange("(c t p) d -> c p t d", p=P, t=TQ)
                with sp.Fori(0, NCH) as c:
                    sp.wait_ge(s["acc_done"], EX * TQ * (c + 1))
                    sp.dma_start(ov[c], outb[:, :, :]).then_inc(s["out_stored"], 16)
                sp.wait_ge(s["out_stored"], 16 * NCH)

            @block.gpsimd
            def _(pool):
                g = nc.gpsimd
                for e in range(EX):
                    g.memset(rank[:, e:e + 1], float(EX - e))
                last = g.memset(euler[:, :], math.e)
                last.then_inc(s["rank_done"], 1)

                def rsqrt_z(p):
                    wait_alone(pool, s["vez_done"], p + 1)
                    if not is_first(p):
                        wait_alone(pool, s["hz_done"], TQ * p)
                    g.tensor_tensor(rstdz[:, :], vez[:, :], power[:, 0:TQ], ALU.pow).then_inc(s["rstdz_done"], 1)

                def chunk(c):
                    wait_alone(pool, s["gap_done"], c + 1)
                    g.tensor_tensor(egap[:, :], euler[:, :], gap[:, :], ALU.pow).then_inc(s["egap_done"], 1)
                    wait_alone(pool, s["resid_done"], c + 1)
                    if not is_first(c):
                        wait_alone(pool, s["acc_done"], EX * TQ * c)
                    g.tensor_copy(base[:, :, :], xs[:, bass.ds(c * TQ, TQ), :]).then_inc(s["base_ready"], 1)
                    if not is_last(c):
                        rsqrt_z(c + 1)
                rsqrt_z(0)
                chunks(chunk)(pool)

            @block.scalar
            def _(act):
                a = nc.scalar

                def fetch(p):
                    if not is_first(p):
                        act.wait_ge(s["att_turned"], p)
                    a.copy(attc[:, :, :], att[:, bass.ds(TQ * p, TQ), :]).then_inc(s["attc_done"], 1)

                def att_copy(p):
                    act.wait_ge(s["att_turned"], p + 1)
                    if not is_first(p):
                        act.wait_ge(s["wo2_done"], p)
                    a.copy(attT[:, :], pA[:, :]).then_inc(s["attT_done"], 1)

                def scale_shift(p):
                    act.wait_ge(s["hz_turned"], p + 1)
                    if not is_first(p):
                        act.wait_ge(s["gate_done"], p)
                        act.wait_ge(s["h2T_done"], p)
                    a.activation(hzT[:, :], pA[:, :], ACT.Identity, bias=t2_c, scale=s2_c).then_inc(s["hzT_done"], 1)

                prep = {0: [fetch], 2: [att_copy], 12: [scale_shift]}

                def chunk(c):
                    for u in range(NU):
                        act.wait_ge(s["up_done"], NU * c + u + 1)
                        if not (is_first(c) and u < 2):
                            act.wait_ge(s["hid_done"], NU * c + u - 1)
                        a.activation(silu[u % 2][:, :], gb[u % 2][:, :], ACT.Silu).then_inc(s["silu_done"], 1)
                        prepare(prep, c, u)
                fetch(0)
                act.wait_ge(ffn_in, 16 * 5)
                for w, head in ((w1_s, w1_head), (w2_s, w2_head)):
                    a.copy(head[:, :, :].bitcast(fp32r), w[:, :, :]).then_inc(s["w_head_done"], 1)
                att_copy(0)
                scale_shift(0)
                chunks(chunk)(act)

            @block.vector
            def _(dve):
                v = nc.vector

                def make_z(p):
                    o = pB[:, :].rearrange("p (t d) -> p t d", t=TQ)
                    toks = bass.ds(TQ * p, TQ)
                    dve.wait_ge(s["wo2_done"], p + 1)
                    v.tensor_tensor(z[:, :, :], o, yb[:, toks, :], ALU.add).then_inc(s["z_done"], 1)
                    v.tensor_tensor(xs[:, toks, :], o, xs[:, toks, :], ALU.add).then_inc(s["resid_done"], 1)

                def z_stats(p):
                    wait_alone(dve, s["z_done"], p + 1)
                    for t in range(TQ):
                        v.bn_stats(bnz[:, t, :], z[:, t, :]).then_inc(s["bnz_done"], 1)

                def z_moments(p):
                    wait_alone(dve, s["bnz_done"], TQ * (p + 1))
                    for t in range(TQ):
                        v.bn_aggr(stz[:, t, :], bnz[:, t, :]).then_inc(s["stz_done"], 1)
                    wait_alone(dve, s["stz_done"], TQ * (p + 1))
                    v.tensor_scalar(vez[:, :], stz[:, :, 1], EPS, None, ALU.add).then_inc(s["vez_done"], 1)

                def norm_z(p):
                    wait_alone(dve, s["rstdz_done"], p + 1)
                    if not is_first(p):
                        wait_alone(dve, s["hz_turned"], p)
                    for t in range(TQ):
                        v.tensor_scalar(hz[:, t, :], z[:, t, :], stz[:, t, 0:1], rstdz[:, t:t + 1],
                                        ALU.subtract, ALU.mult).then_inc(s["hz_done"], 1)

                def head_of_h2(p):
                    dve.wait_ge(s["hzT_done"], p + 1)
                    v.tensor_copy(h2_head[:, bass.ds(p * Q, Q)].bitcast(fp32r), hzT[:, :]).then_inc(s["head_done"], 1)

                def rest_of_h2(p):
                    head, rest_ = (a[:, bass.ds(p * Q, Q)] for a in (h2_head, h2_rest))
                    dve.wait_ge(s["head_done"], p + 1)
                    v.tensor_tensor(rest_.bitcast(fp32r), hzT[:, :], head, ALU.subtract).then_inc(s["h2T_done"], 1)

                def keep_logits(p):
                    dve.wait_ge(s["gate_done"], p + 1)
                    v.tensor_copy(logits[:, :, :], pB[:, 0:TQ * EX].rearrange("p (t e) -> p t e", e=EX))\
                        .then_inc(s["logits_done"], 1)

                rk = rank[:, :].unsqueeze(1).to_broadcast([P, TQ, EX])

                def wide(a):
                    return a.unsqueeze(2).to_broadcast([P, TQ, EX])

                def choose(scores, m, onehot):
                    return [lambda: v.tensor_reduce(best[:, m, :], scores, X, ALU.max),
                            lambda: v.tensor_tensor(sel[:, :, :], scores, wide(best[:, m, :]), ALU.is_equal),
                            lambda: v.tensor_tensor(sel[:, :, :], sel[:, :, :], rk, ALU.mult),
                            lambda: v.tensor_reduce(pick[:, :], sel[:, :, :], X, ALU.max),
                            lambda: v.tensor_tensor(onehot[:, :, :], rk, wide(pick[:, :]), ALU.is_equal)]
                choosing = choose(logits[:, :, :], 0, oh1) + [
                    lambda: v.tensor_scalar(sel[:, :, :], oh1[:, :, :], -1.0, 1.0, ALU.mult, ALU.add),
                    lambda: v.tensor_tensor(rest[:, :, :], logits[:, :, :], sel[:, :, :], ALU.mult),
                    lambda: v.tensor_scalar(sel[:, :, :], oh1[:, :, :], MASKED, None, ALU.mult),
                    lambda: v.tensor_tensor(rest[:, :, :], rest[:, :, :], sel[:, :, :], ALU.add),
                ] + choose(rest[:, :, :], 1, oh2)
                weighting = [
                    lambda: v.tensor_scalar(eone[:, :], egap[:, :], 1.0, None, ALU.add),
                    lambda: v.reciprocal(pr[:, 0, :], eone[:, :]),
                    lambda: v.tensor_tensor(pr[:, 1, :], pr[:, 0, :], egap[:, :], ALU.mult),
                    lambda: v.tensor_tensor(oh1[:, :, :], oh1[:, :, :], wide(pr[:, 0, :]), ALU.mult),
                    lambda: v.tensor_tensor(oh2[:, :, :], oh2[:, :, :], wide(pr[:, 1, :]), ALU.mult)]
                STEPS = len(choosing) + len(weighting)

                def gating(p, steps, done):
                    for n, f in enumerate(steps):
                        f().then_inc(s["gating_step"], 1)
                        wait_alone(dve, s["gating_step"], STEPS * p + done + n + 1)

                def score_gap(p):
                    v.tensor_tensor(gap[:, :], best[:, 1, :], best[:, 0, :], ALU.subtract).then_inc(s["gap_done"], 1)

                def weigh(p):
                    wait_alone(dve, s["egap_done"], p + 1)
                    gating(p, weighting, len(choosing))
                def add_weights(p):
                    v.tensor_tensor(wc[:, :, :], oh1[:, :, :], oh2[:, :, :], ALU.add).then_inc(s["wc_done"], 1)

                def choosing_steps(first_step, end):
                    return lambda p: gating(p, choosing[first_step:end], first_step)

                def logits_kept(p):
                    wait_alone(dve, s["logits_done"], p + 1)
                prep = {4: [make_z], 5: [z_stats], 6: [z_moments], 10: [norm_z], 13: [head_of_h2], 14: [rest_of_h2],
                        15: [keep_logits],
                        NU: [logits_kept, choosing_steps(0, 10)], NU + 1: [choosing_steps(10, 14), score_gap],
                        NU + 2: [weigh, add_weights]}

                def hidden(c, u):
                    e, k = divmod(u, KH)
                    dve.wait_ge(s["silu_done"], NU * c + u + 1)
                    if k == 0 and not (is_first(c) and e < 2):
                        dve.wait_ge(s["down_done"], EX * c + e - 1)
                    v.tensor_tensor(hid[e % 2][:, k, :], ub[u % 2][:, :], silu[u % 2][:, :], ALU.mult)\
                        .then_inc(s["hid_done"], 1)

                def combine(c, e):
                    dve.wait_ge(s["down_done"], EX * c + e + 1)
                    if e == 0:
                        dve.wait_ge(s["base_ready"], c + 1)
                        dve.wait_ge(s["wc_done"], c + 1)
                    if e > 0:
                        dve.wait_ge(s["acc_done"], TQ * (EX * c + e))
                    if e == EX - 1 and not is_first(c):
                        dve.wait_ge(s["out_stored"], 16 * c)
                    src = base if e == 0 else acc
                    dst = outb if e == EX - 1 else acc
                    for t in range(TQ):
                        v.scalar_tensor_tensor(dst[:, t, :], ob[e % 2][:, t * P:(t + 1) * P], wc[:, t, e:e + 1],
                                               src[:, t, :], ALU.mult, ALU.add).then_inc(s["acc_done"], 1)

                def chunk(c):
                    for u in range(NU):
                        hidden(c, u)
                        if u == 1 and not is_first(c):
                            combine(c - 1, EX - 1)
                        if u % KH == KH - 1 and u > KH:
                            combine(c, u // KH - 1)
                        prepare(prep, c, u)
                dve.wait_ge(s["rank_done"], 1)
                for n, (w, head, rest_) in enumerate(((w1_s, w1_head, w1_rest), (w2_s, w2_head, w2_rest))):
                    dve.wait_ge(s["w_head_done"], n + 1)
                    v.tensor_tensor(rest_[:, :, :].bitcast(fp32r), w[:, :, :], head[:, :, :], ALU.subtract)\
                        .then_inc(s["w_rest_done"], 1)
                prepare_all(prep, 0)
                chunks(chunk)(dve)
                combine(NCH - 1, EX - 1)

            @block.tensor
            def _(pe):
                t_ = nc.tensor

                def att_turn(p):
                    pe.wait_ge(s["attc_done"], p + 1)
                    if not is_first(p):
                        pe.wait_ge(s["hzT_done"], p)
                    for t in range(TQ):
                        last = t_.transpose(pA[:, t * P:(t + 1) * P], attc[:, t, :], ident[:, :])
                    last.then_inc(s["att_turned"], 1)

                def att_out(p):
                    pe.wait_ge(s["attT_done"], p + 1)
                    if not is_first(p):
                        pe.wait_ge(s["logits_done"], p)
                    for t in range(TQ):
                        last = t_.matmul(pB[:, t * P:(t + 1) * P], attT[:, t * P:(t + 1) * P], wo_s[:, :],
                                         start=True, stop=True)
                    last.then_inc(s["wo2_done"], 1)

                def z_turn(p):
                    pe.wait_ge(s["hz_done"], TQ * (p + 1))
                    pe.wait_ge(s["attT_done"], p + 1)
                    for t in range(TQ):
                        last = t_.transpose(pA[:, t * P:(t + 1) * P], hz[:, t, :], ident[:, :])
                    last.then_inc(s["hz_turned"], 1)

                def gate(p):
                    pe.wait_ge(s["hzT_done"], p + 1)
                    pe.wait_ge(s["resid_done"], p + 1)
                    for t in range(TQ):
                        last = t_.matmul(pB[:, t * EX:(t + 1) * EX], hzT[:, t * P:(t + 1) * P], gate_s[:, :],
                                         start=True, stop=True)
                    last.then_inc(s["gate_done"], 1)
                prep = {1: [att_turn], 3: [att_out], 12: [z_turn], 14: [gate]}

                def up(c, e):
                    if e == 0:
                        pe.wait_ge(s["h2T_done"], c + 1)
                    for k in range(KH):
                        u = e * KH + k
                        if not (is_first(c) and u < 2):
                            pe.wait_ge(s["hid_done"], NU * c + u - 1)
                        for o, w_head, w_rest in ((gb, w1_head, w1_rest), (ub, w2_head, w2_rest)):
                            products = ((w_head, h2_head), (w_head, h2_rest), (w_rest, h2_head))
                            for n, (w, h) in enumerate(products):
                                last = t_.matmul(o[u % 2][:, :], w[:, e, k * P:(k + 1) * P].bitcast(fp32r),
                                                 h[:, bass.ds(c * Q, Q)].bitcast(fp32r), start=n == 0, stop=n == 2)
                        last.then_inc(s["up_done"], 1)
                        prepare(prep, c, u)

                def down(c, e):
                    pe.wait_ge(s["hid_done"], KH * (EX * c + e + 1))
                    if not (is_first(c) and e < 2):
                        pe.wait_ge(s["acc_done"], TQ * (EX * c + e - 1))
                    for t in range(TQ):
                        for k in range(KH):
                            last = t_.matmul(ob[e % 2][:, t * P:(t + 1) * P], hid[e % 2][:, k, t * P:(t + 1) * P],
                                             w3_s[:, e, k, :], start=k == 0, stop=k == KH - 1)
                    last.then_inc(s["down_done"], 1)

                def chunk(c):
                    for e in range(EX):
                        up(c, e)
                        if e > 0:
                            down(c, e - 1)
                        elif not is_first(c):
                            down(c - 1, EX - 1)
                pe.wait_ge(ffn_in, 16 * 5)
                prepare_all(prep, 0)
                pe.wait_ge(s["w_rest_done"], 2)
                chunks(chunk)(pe)
                down(NCH - 1, EX - 1)


_INS = ['x', 'Wq', 'bq', 'Wk', 'bk', 'Wv', 'bv', 'Wo', 'bo']
_FFN = ['ln1_scale', 'ln1_shift', 'wq', 'wk', 'wv', 'wo', 'bo', 'ln2_scale', 'ln2_shift', 'gate_w', 'w1', 'w2', 'w3']
_ALL = ['L0_attn_' + n for n in _INS] + ['L0_ffn_' + n for n in _FFN]


def kernel(**inputs):
    import numpy as _np
    import concourse.bacc as _bacc
    from concourse import mybir as _mybir
    from concourse.bass_utils import run_bass_kernel_spmd as _run

    nc = _bacc.Bacc("TRN2", target_bir_lowering=False, num_devices=1)
    arrays, args = {}, []
    for name in _ALL:
        a = _np.ascontiguousarray(inputs[name])
        arrays[f"in_{name}"] = a
        args.append(nc.dram_tensor(f"in_{name}", a.shape, _mybir.dt.from_np(a.dtype), kind="ExternalInput").ap())
    shape = inputs['L0_attn_x'].shape
    args.append(nc.dram_tensor("out_dram", shape, _mybir.dt.float32, kind="ExternalOutput").ap())
    preln_layer_kernel(nc, *args)
    r = _run(nc, [arrays], core_ids=[0])
    return r.results[0]["out_dram"]
```
